# Optimizing a Trainium2 kernel written in Bass

```python
import numpy as np
import jax
import jax.numpy as jnp

def _softmax(x, axis=-1):
    return jax.nn.softmax(x, axis=axis)

def _gelu(x):
    return jax.nn.gelu(x, approximate=True)

def _silu(x):
    return jax.nn.silu(x)

def _sigmoid(x):
    return jax.nn.sigmoid(x)

def _layernorm(x, axis=-1, eps=1e-05):
    m = jnp.mean(x, axis=axis, keepdims=True)
    v = jnp.var(x, axis=axis, keepdims=True)
    return (x - m) / jnp.sqrt(v + eps)

def _scatter_add(tgt, idx, src, axis=0):
    return tgt.at[idx].add(src)

def _segment_sum(src, seg, n):
    return jax.ops.segment_sum(src, seg, n)
kernel_name = 'mk_adaln_ffn_d2_seqx_r8_dc1789'

def setup_inputs(seed: int=0):
    np.random.seed(seed)
    _w = jnp.asarray

    def _rec_inputs():
        import jax
        import jax.numpy as jnp
        _rk = jax.random.key(seed)
        x = -7.109e-05 + 0.9999 * jax.random.normal(jax.random.fold_in(_rk, 1), (32, 32, 256), jnp.float32)
        _lenS = 32 - jax.random.randint(jax.random.fold_in(_rk, 7), (32,), 0, max(1, 32 // 4) + 1, jnp.int32)
        _lenS2 = 32 - jax.random.randint(jax.random.fold_in(_rk, 8), (32,), 0, max(1, 32 // 4) + 1, jnp.int32)
        itok_B_1_198 = jax.random.randint(jax.random.fold_in(_rk, 11), (32,), 1, 199, jnp.int32)
        itok_B_0_7 = jax.random.randint(jax.random.fold_in(_rk, 12), (32,), 0, 8, jnp.int32)
        return (x, itok_B_1_198, itok_B_0_7)
    x, itok_B_1_198, itok_B_0_7 = _rec_inputs()

    def _L0_cond_setup():
        import jax, jax.numpy as jnp
        import numpy as np
        B, C, T = (128, 32, 256)
        S, D = (200, 32)
        key = jax.random.key(seed)
        k1, k2, k3 = jax.random.split(key, 3)
        x = jax.random.normal(k1, (B, C, T), dtype=jnp.float32)
        conditions = jax.random.randint(k2, (B,), 0, S, dtype=jnp.int64)
        weights = jax.random.normal(k3, (S, C, D), dtype=jnp.float32) / jnp.sqrt(jnp.float32(C))
        return {'x': x, 'conditions': conditions, 'weights': weights}
    _L0_cond_all = _L0_cond_setup()
    _L0_cond_in = {k: v for k, v in _L0_cond_all.items() if k in ('weights',)}
    del _L0_cond_all

    def _L0_ffn_setup():
        import jax, jax.numpy as jnp
        import numpy as np
        H = 256
        HQ = 16
        HKV = 4
        D = 128
        E = 32
        K = 4
        I = 128
        ISH = 128
        EPS = 1e-06
        THETA = 10000.0
        NORM_MIN = 1e-12

        def rmsnorm(x, w):
            xf = x.astype(jnp.float32)
            var = jnp.mean(xf * xf, axis=-1, keepdims=True)
            return w * (xf * jax.lax.rsqrt(var + EPS))

        def rotate_half(x):
            x1 = x[..., 0::2]
            x2 = x[..., 1::2]
            return jnp.stack((-x2, x1), axis=-1).reshape(x.shape)
        key = jax.random.key(seed)
        ks = jax.random.split(key, 14)
        s = 0.02
        B, S = (1, 128)
        return {'hidden_states': jax.random.normal(ks[0], (B, S, H), jnp.float32), 'ln1_w': jnp.ones((H,), jnp.float32), 'ln2_w': jnp.ones((H,), jnp.float32), 'wq': jax.random.normal(ks[1], (H, HQ * D), jnp.float32) * s, 'wk': jax.random.normal(ks[2], (H, HKV * D), jnp.float32) * s, 'wv': jax.random.normal(ks[3], (H, HKV * D), jnp.float32) * s, 'wo': jax.random.normal(ks[4], (HQ * D, H), jnp.float32) * s, 'gate_w': jax.random.normal(ks[5], (E, H), jnp.float32) * s, 'bias_e': jnp.zeros((E,), jnp.float32), 'weg': jax.random.normal(ks[6], (E, H, I), jnp.float32) * s, 'weu': jax.random.normal(ks[7], (E, H, I), jnp.float32) * s, 'wed': jax.random.normal(ks[8], (E, I, H), jnp.float32) * s, 'wsg': jax.random.normal(ks[9], (H, ISH), jnp.float32) * s, 'wsu': jax.random.normal(ks[10], (H, ISH), jnp.float32) * s, 'wsd': jax.random.normal(ks[11], (ISH, H), jnp.float32) * s}
    _L0_ffn_all = _L0_ffn_setup()
    _L0_ffn_in = {k: v for k, v in _L0_ffn_all.items() if k in ('ln1_w', 'ln2_w', 'wq', 'wk', 'wv', 'wo', 'gate_w', 'bias_e', 'weg', 'weu', 'wed', 'wsg', 'wsu', 'wsd')}
    del _L0_ffn_all

    def _L1_cond_setup():
        import jax, jax.numpy as jnp
        import numpy as np
        B, C, D, T, N_SUBJECTS = (128, 32, 32, 256, 8)
        key = jax.random.key(seed)
        kx, ks, kw = jax.random.split(key, 3)
        x = jax.random.normal(kx, (B, C, T), dtype=jnp.float32)
        subjects = jax.random.randint(ks, (B,), 0, N_SUBJECTS, dtype=jnp.int64)
        weights = jax.random.normal(kw, (N_SUBJECTS, C, D), dtype=jnp.float32) * (1.0 / C ** 0.5)
        return {'x': x, 'subjects': subjects, 'weights': weights}
    _L1_cond_all = _L1_cond_setup()
    _L1_cond_in = {k: v for k, v in _L1_cond_all.items() if k in ('weights',)}
    del _L1_cond_all

    def _L1_ffn_setup():
        import jax, jax.numpy as jnp
        import numpy as np
        B, S, D, K, R = (4, 256, 256, 8, 64)
        key = jax.random.key(seed)
        ks = jax.random.split(key, 7)
        x = jax.random.normal(ks[0], (B, S, D), dtype=jnp.float32)
        U = jax.random.normal(ks[1], (K, D, R), dtype=jnp.float32) * 0.02
        V = jax.random.normal(ks[2], (K, R, D), dtype=jnp.float32) * 0.02
        W1 = jax.random.normal(ks[3], (D, D), dtype=jnp.float32) * 0.02
        b1 = jnp.zeros((D,), dtype=jnp.float32)
        W2 = jax.random.normal(ks[4], (D, K), dtype=jnp.float32) * 0.02
        b2 = jnp.zeros((K,), dtype=jnp.float32)
        return {'x': x, 'U': U, 'V': V, 'W1': W1, 'b1': b1, 'W2': W2, 'b2': b2}
    _L1_ffn_all = _L1_ffn_setup()
    _L1_ffn_in = {k: v for k, v in _L1_ffn_all.items() if k in ('U', 'V', 'W1', 'b1', 'W2', 'b2')}
    del _L1_ffn_all
    return {'x': x, 'itok_B_1_198': itok_B_1_198, 'itok_B_0_7': itok_B_0_7, 'L0_cond_weights': _L0_cond_in['weights'], 'L0_ffn_ln1_w': _L0_ffn_in['ln1_w'], 'L0_ffn_ln2_w': _L0_ffn_in['ln2_w'], 'L0_ffn_wq': _L0_ffn_in['wq'], 'L0_ffn_wk': _L0_ffn_in['wk'], 'L0_ffn_wv': _L0_ffn_in['wv'], 'L0_ffn_wo': _L0_ffn_in['wo'], 'L0_ffn_gate_w': _L0_ffn_in['gate_w'], 'L0_ffn_bias_e': _L0_ffn_in['bias_e'], 'L0_ffn_weg': _L0_ffn_in['weg'], 'L0_ffn_weu': _L0_ffn_in['weu'], 'L0_ffn_wed': _L0_ffn_in['wed'], 'L0_ffn_wsg': _L0_ffn_in['wsg'], 'L0_ffn_wsu': _L0_ffn_in['wsu'], 'L0_ffn_wsd': _L0_ffn_in['wsd'], 'L1_cond_weights': _L1_cond_in['weights'], 'L1_ffn_U': _L1_ffn_in['U'], 'L1_ffn_V': _L1_ffn_in['V'], 'L1_ffn_W1': _L1_ffn_in['W1'], 'L1_ffn_b1': _L1_ffn_in['b1'], 'L1_ffn_W2': _L1_ffn_in['W2'], 'L1_ffn_b2': _L1_ffn_in['b2']}

def reference(x, itok_B_1_198, itok_B_0_7, L0_cond_weights, L0_ffn_ln1_w, L0_ffn_ln2_w, L0_ffn_wq, L0_ffn_wk, L0_ffn_wv, L0_ffn_wo, L0_ffn_gate_w, L0_ffn_bias_e, L0_ffn_weg, L0_ffn_weu, L0_ffn_wed, L0_ffn_wsg, L0_ffn_wsu, L0_ffn_wsd, L1_cond_weights, L1_ffn_U, L1_ffn_V, L1_ffn_W1, L1_ffn_b1, L1_ffn_W2, L1_ffn_b2):
    import jax
    import jax.numpy as jnp

    def _L0_cond_ref(x, conditions, weights):
        import jax, jax.numpy as jnp
        import numpy as np
        B, C, T = (128, 32, 256)
        S, D = (200, 32)
        w = weights[conditions]
        return jnp.einsum('bct,bcd->bdt', x, w)

    def _L0_ffn_ref(hidden_states, ln1_w, ln2_w, wq, wk, wv, wo, gate_w, bias_e, weg, weu, wed, wsg, wsu, wsd):
        import jax, jax.numpy as jnp
        import numpy as np
        H = 256
        HQ = 16
        HKV = 4
        D = 128
        E = 32
        K = 4
        I = 128
        ISH = 128
        EPS = 1e-06
        THETA = 10000.0
        NORM_MIN = 1e-12

        def rmsnorm(x, w):
            xf = x.astype(jnp.float32)
            var = jnp.mean(xf * xf, axis=-1, keepdims=True)
            return w * (xf * jax.lax.rsqrt(var + EPS))

        def rotate_half(x):
            x1 = x[..., 0::2]
            x2 = x[..., 1::2]
            return jnp.stack((-x2, x1), axis=-1).reshape(x.shape)
        B, S, _ = hidden_states.shape
        resid = hidden_states
        x = rmsnorm(hidden_states, ln1_w)
        q = (x @ wq).reshape(B, S, HQ, D).transpose(0, 2, 1, 3)
        k = (x @ wk).reshape(B, S, HKV, D).transpose(0, 2, 1, 3)
        v = (x @ wv).reshape(B, S, HKV, D).transpose(0, 2, 1, 3)
        pos = jnp.arange(S, dtype=jnp.float32)
        inv_freq = 1.0 / THETA ** (jnp.arange(0, D, 2, dtype=jnp.float32) / D)
        ang = pos[:, None] * inv_freq[None, :]
        cos = jnp.repeat(jnp.cos(ang), 2, axis=-1)[None, None]
        sin = jnp.repeat(jnp.sin(ang), 2, axis=-1)[None, None]
        q = q * cos + rotate_half(q) * sin
        k = k * cos + rotate_half(k) * sin
        k = jnp.repeat(k, HQ // HKV, axis=1)
        v = jnp.repeat(v, HQ // HKV, axis=1)
        scores = jnp.einsum('bhqd,bhkd->bhqk', q, k) / jnp.sqrt(jnp.float32(D))
        causal = jnp.tril(jnp.ones((S, S), dtype=bool))
        scores = jnp.where(causal, scores, jnp.float32(-1000000000.0))
        attn = jax.nn.softmax(scores, axis=-1)
        o = jnp.einsum('bhqk,bhkd->bhqd', attn, v).transpose(0, 2, 1, 3).reshape(B, S, HQ * D)
        x = resid + o @ wo
        resid2 = x
        xn = rmsnorm(x, ln2_w)
        T = B * S
        xf = xn.reshape(T, H).astype(jnp.float32)
        router_logits = xf @ gate_w.T
        probs = jax.nn.softmax(router_logits, axis=-1)
        _, sel = jax.lax.top_k(probs + bias_e, K)
        rw = jnp.take_along_axis(probs, sel, axis=-1)
        rw = rw / jnp.maximum(jnp.sum(rw, axis=-1, keepdims=True), NORM_MIN)
        cw = jnp.zeros((T, E), jnp.float32).at[jnp.arange(T)[:, None], sel].set(rw)
        g = jnp.einsum('th,ehi->tei', xf, weg)
        u = jnp.einsum('th,ehi->tei', xf, weu)
        hmid = jax.nn.silu(g) * u * cw[:, :, None]
        moe_y = jnp.einsum('tei,eih->th', hmid, wed).reshape(B, S, H)
        shared = jax.nn.silu(xn @ wsg) * (xn @ wsu) @ wsd
        return resid2 + moe_y + shared

    def _L1_cond_ref(x, subjects, weights):
        import jax, jax.numpy as jnp
        import numpy as np
        B, C, D, T, N_SUBJECTS = (128, 32, 32, 256, 8)
        w = weights[subjects]
        out = jnp.einsum('bct,bcd->bdt', x, w)
        return out

    def _L1_ffn_ref(x, U, V, W1, b1, W2, b2):
        import jax, jax.numpy as jnp
        import numpy as np
        B, S, D, K, R = (4, 256, 256, 8, 64)
        h = jax.nn.relu(jnp.einsum('bsd,de->bse', x, W1) + b1)
        alpha = jax.nn.softmax(jnp.einsum('bse,ek->bsk', h, W2) + b2, axis=-1)
        vx = jnp.einsum('krd,bsd->bskr', V, x)
        uvx = jnp.einsum('kdr,bskr->bskd', U, vx)
        out = jnp.einsum('bsk,bskd->bsd', alpha, uvx)
        return out
    x = x + _L0_ffn_ref(_L0_cond_ref(x, itok_B_1_198, L0_cond_weights), L0_ffn_ln1_w, L0_ffn_ln2_w, L0_ffn_wq, L0_ffn_wk, L0_ffn_wv, L0_ffn_wo, L0_ffn_gate_w, L0_ffn_bias_e, L0_ffn_weg, L0_ffn_weu, L0_ffn_wed, L0_ffn_wsg, L0_ffn_wsu, L0_ffn_wsd)
    x = x + _L1_ffn_ref(_L1_cond_ref(x, itok_B_0_7, L1_cond_weights), L1_ffn_U, L1_ffn_V, L1_ffn_W1, L1_ffn_b1, L1_ffn_W2, L1_ffn_b2)
    return x

_drawn_inputs = setup_inputs


def setup_inputs(seed=0):
    import zlib

    import numpy as np

    out = dict(_drawn_inputs(seed))
    spreads = {'L0_ffn_ln1_w': (1.0, 0.6),
     'L0_ffn_ln2_w': (1.0, 0.6),
     'L0_ffn_bias_e': (0.0, 0.8),
     'L1_ffn_b1': (0.0, 0.8),
     'L1_ffn_b2': (0.0, 2.0)}
    factors = {'L0_ffn_wq': 7.131,
     'L0_ffn_wk': 7.164,
     'L0_ffn_gate_w': 8.0,
     'L0_ffn_weg': 8.0,
     'L0_ffn_weu': 8.0,
     'L0_ffn_wed': 8.0,
     'L0_ffn_wsg': 6.026,
     'L0_ffn_wsu': 5.911,
     'L0_ffn_wsd': 5.859,
     'L1_cond_weights': 3.093,
     'L1_ffn_U': 3.095,
     'L1_ffn_V': 3.099,
     'L1_ffn_W1': 8.0,
     'L1_ffn_W2': 8.0}
    for name, (base, spread) in spreads.items():
        noise = np.random.default_rng([zlib.crc32(name.encode()), seed]).standard_normal(out[name].shape)
        drawn = base * np.exp(spread * noise) if base else spread * noise
        out[name] = jnp.asarray(drawn.astype(out[name].dtype))
    for name, factor in factors.items():
        out[name] = (out[name] * factor).astype(out[name].dtype)
    return out
```

```python
import numpy as np
import concourse.bass as bass
from concourse import mybir
from contextlib import ExitStack

B, S, H = 32, 32, 256
TOK = B * S
P = 128
NT = TOK // P
BT = P // S
HC = H // P
HQ, HKV, D = 16, 4, 128
GQ = HQ // HKV
NPAIR = HKV // 2
FR = D // 2
NC = 2
CT = NT // NC
CW = TOK // NC
E, K, I = 32, 4, 128
NSUB = 8
R = 64
KR = NSUB * R
MOE_TILES = TOK * K // P + E
EPS = 1e-6
NORM_MIN = 1e-12
THETA = 10000.0
SM_SCALE = float(1.0 / np.sqrt(np.float32(D)))
MASKED = float(-1e9 * np.sqrt(D))
RSQRT_SEED = 1597463007.0

C_IDENT = 0
C_COS = C_IDENT + P
C_SIN = C_COS + S
C_MASK = C_SIN + 2 * S
C_TRI = C_MASK + S
C_IOTA = C_TRI + P
C_ROW0 = C_IOTA + E
C_PART = C_ROW0 + E
C_PMOD = C_PART + 1
C_TOK = C_PMOD + 1
C_END = C_TOK + NT


def constants():
    c = np.zeros((P, C_END), np.float32)
    p = np.arange(P)
    c[:, C_IDENT:C_COS] = np.eye(P)
    inv = 1.0 / np.float32(THETA) ** (np.arange(0, D, 2, dtype=np.float32) / np.float32(D))
    ang = np.arange(S, dtype=np.float32)[None, :] * inv.astype(np.float32)[p % FR][:, None]
    c[:, C_COS:C_SIN] = np.cos(ang)
    c[:, C_SIN:C_SIN + S] = -np.sin(ang)
    c[:, C_SIN + S:C_MASK] = np.sin(ang)
    c[:, C_MASK:C_TRI] = np.where(np.arange(S)[None, :] <= (p % S)[:, None], 0.0, MASKED)
    c[:, C_TRI:C_IOTA] = p[:, None] < p[None, :]
    c[:, C_IOTA:C_ROW0] = np.arange(E)[None, :]
    c[:, C_ROW0:C_PART] = TOK * np.arange(E)[None, :]
    c[:, C_PART] = p
    c[:, C_PMOD] = p % S
    c[:, C_TOK:C_END] = np.arange(NT)[None, :] * P + p[:, None]
    return c


def build(nc, x, cond0, cond1, w_cond0, w_cond1, consts, ln1, ln2, wq, wk, wv, wo, gate, bias_e,
          weg, weu, wed, wsg, wsu, wsd, u_t, v_t, w1, b1, w2, b2, out):
    F32, BF16, I32, U32 = mybir.dt.float32, mybir.dt.bfloat16, mybir.dt.int32, mybir.dt.uint32
    ALU, ACT, AX = mybir.AluOpType, mybir.ActivationFunctionType, mybir.AxisListType.X

    ctx = ExitStack()
    with ctx:
        def sb(name, shape, dt=F32):
            return ctx.enter_context(nc.sbuf_tensor(name, shape, dt))

        def sem(name):
            return ctx.enter_context(nc.semaphore(name))

        cst = sb("cst", [P, C_END])
        h_sb = sb("h_sb", [P, NT, H])
        xs = sb("xs", [P, NT, H])
        xT = sb("xT", [P, HC, TOK])
        cond_sb = sb("cond_sb", [P, 2, NT], I32)
        cidx = sb("cidx", [P, 2, NT], I32)
        wbd = sb("wbd", [P, 2, NT, P])
        ln1_sb = sb("ln1_sb", [P, HC])
        ln2_sb = sb("ln2_sb", [P, H])
        ss = sb("ss", [P, NT])
        rs = sb("rs", [P, 3, CT])
        gate_sb = sb("gate_sb", [P, HC, E])
        bias_sb = sb("bias_sb", [P, E])
        probs = sb("probs", [P, NT, E])
        biased = sb("biased", [P, NT, E])
        rt = sb("rt", [P, 3, CT])
        top = sb("top", [P, NT, 8])
        top_at = sb("top_at", [P, NT, 8], U32)
        top_f = sb("top_f", [P, NT, K])
        picked = sb("picked", [P, NT, K, E])
        tmp_ke = sb("tmp_ke", [P, CT, K, E])
        w4 = sb("w4", [P, NT, K])
        rw = sb("rw", [P, 2, NT])
        chosen = sb("chosen", [P, NT, E], BF16)
        tri = sb("tri", [P, P], BF16)
        ones = sb("ones", [P, P], BF16)
        rank = sb("rank", [P, NT, E])
        row_of = sb("row_of", [P, NT, E])
        row_f = sb("row_f", [P, NT, K])
        row_i = sb("row_i", [P, NT, K], I32)
        slot_i = sb("slot_i", [P, NT, K], I32)
        tab = sb("tab", [P, 6, E])
        tab_i = sb("tab_i", [P, 2, E], I32)
        col = sb("col", [P, 8])
        src_i = sb("src_i", [P, MOE_TILES], I32)
        tok_i = sb("tok_i", [P, NT], I32)
        zeros_i = sb("zeros_i", [P, P], I32)
        block_i = sb("block_i", [P, 1], I32)
        tile_tok_i = sb("tile_tok_i", [P, P], I32)
        expert_of = sb("expert_of", [1, MOE_TILES], I32)
        wsg_sb = sb("wsg_sb", [P, HC, I])
        wsu_sb = sb("wsu_sb", [P, HC, I])
        wsd_sb = sb("wsd_sb", [P, H])
        sh = sb("sh", [P, CW])
        sizes = dict(wq=HC * NPAIR * GQ * 2 * P, wk=HC * NPAIR * 2 * P, wv=HC * HKV * D, rope=2 * 2 * 2 * CW,
                     q=2 * 2 * CW * GQ, k=2 * 2 * CW * 2, v=CT * HKV * D, pr=2 * 512, prT=2 * 512, wo=HQ * H, oT=HQ * CW)
        arena = sb("arena", [P, sum(sizes.values())])
        starts, at = {}, 0
        for name, size in sizes.items():
            starts[name] = at
            at += size

        def part(name):
            return arena[:, starts[name]:starts[name] + sizes[name]]

        wq_sb = part("wq").rearrange("p (c g j e n) -> p c g j e n", c=HC, g=NPAIR, j=GQ, e=2)
        wk_sb = part("wk").rearrange("p (c g e n) -> p c g e n", c=HC, g=NPAIR, e=2)
        wv_sb = part("wv").rearrange("p (c n) -> p c n", c=HC)
        wo_sb = part("wo").rearrange("p (h n) -> p h n", h=HQ)
        rope_cs = part("rope").rearrange("p (w n e t) -> p w n e t", w=2, n=2, e=2)
        rope_c, rope_s = rope_cs[:, 0], rope_cs[:, 1]
        q_sb = part("q").rearrange("p (u e b j s) -> p u e b j s", u=2, e=2, b=CT * BT, j=GQ)
        k_sb = part("k").rearrange("p (u e b g s) -> p u e b g s", u=2, e=2, b=CT * BT, g=2)
        v_sb = part("v").rearrange("p (i n) -> p i n", i=CT)
        pr = part("pr").rearrange("p (n i s b k) -> p n i s b k", n=2, i=2, s=2, b=BT)
        prT = part("prT").rearrange("p (n i s q) -> p n i s q", n=2, i=2, s=2)
        oT = part("oT").rearrange("p (h t) -> p h t", h=HQ)
        GU = E * HC * 2 * I
        wgu_sb = arena[:, 0:GU].rearrange("p (e c m n) -> p e c m n", e=E, c=HC, m=2)
        wed_sb = arena[:, GU:GU + E * H].rearrange("p (e n) -> p e n", e=E)
        GU_EARLY = starts["q"] // (HC * 2 * I)
        assert GU + E * H <= starts["pr"]
        st = sb("st", [P, 2, 3, CT * BT])
        XB = 4
        x_first = arena[:, starts["oT"]:starts["oT"] + NT * H].rearrange("p (i t) -> p i t", i=NT)
        wst = arena[:, starts["oT"] + NT * H:starts["oT"] + NT * (H + 2 * S)].rearrange("p (m i s) -> p m i s", m=2, s=S)
        free = [starts["pr"]]

        def late(n):
            free[0] += n
            assert free[0] <= at
            return arena[:, free[0] - n:free[0]]

        xg = late(XB * H).rearrange("p (n t) -> p n t", n=XB)
        xgT = late(2 * H).rearrange("p (n c t) -> p n c t", n=2, c=HC)
        th = late(2 * I).rearrange("p (n t) -> p n t", n=2)
        ga = late(2 * I).rearrange("p (n t) -> p n t", n=2)
        hm = late(2 * I).rearrange("p (n t) -> p n t", n=2)
        hmT = late(2 * P).rearrange("p (n t) -> p n t", n=2)
        ye = late(XB * H).rearrange("p (n t) -> p n t", n=XB)
        yg = late(2 * K * H).rearrange("p (n k t) -> p n k t", n=2, k=K)
        zT = late(2 * H).rearrange("p (n c t) -> p n c t", n=2, c=HC)
        hT = late(2 * H).rearrange("p (n c t) -> p n c t", n=2, c=HC)
        al = late(2 * 4 * NSUB).rearrange("p (n m t) -> p n m t", n=2, m=4)
        vx = late(2 * KR).rearrange("p (n t) -> p n t", n=2)
        vxT = late(2 * KR).rearrange("p (n m t) -> p n m t", n=2, m=KR // P)
        tile_tok = late(P)
        slot_f = late(NT * K).rearrange("p (i k) -> p i k", k=K)
        x_again = late(NT * H).rearrange("p (i t) -> p i t", i=NT)
        ut_sb = late(KR // P * H).rearrange("p (m n) -> p m n", n=H)
        vt_sb = late(HC * KR).rearrange("p (c n) -> p c n", c=HC)
        w1_sb = late(HC * H).rearrange("p (c n) -> p c n", c=HC)
        b1_sb = late(HC)
        w2_sb = late(HC * NSUB).rearrange("p (c n) -> p c n", c=HC)
        b2_sb = late(NSUB)

        xd = nc.dram_tensor("normed_tokens", (TOK, H), F32, kind="Internal").ap()
        token_map = nc.dram_tensor("token_map", (E * TOK, 1), I32, kind="Internal").ap()
        yd = nc.dram_tensor("expert_out", (MOE_TILES * P, H), F32, kind="Internal").ap()

        ps = ctx.enter_context(nc.psum_tensor("ps", [P, 8, 512], F32))

        ident = cst[:, C_IDENT:C_COS]
        cosT = cst[:, C_COS:C_SIN]
        sinT = cst[:, C_SIN:C_MASK].rearrange("p (e s) -> p e s", e=2)
        mask = cst[:, C_MASK:C_TRI]

        ld_first = sem("ld_first")
        ld_qkv = sem("ld_qkv")
        ld_wo = sem("ld_wo")
        cidx_ready = sem("cidx_ready")
        wst_loaded = [sem(f"wst_loaded{m}") for m in range(2)]
        wbd_ready = sem("wbd_ready")
        ring_filled = sem("ring_filled")
        act_freed = sem("act_freed")
        dve_freed = sem("dve_freed")
        dve_step = sem("dve_step")
        xs_ready = sem("xs_ready")
        k_zeroed = sem("k_zeroed")
        rope_prod = sem("rope_prod")
        rope_done = sem("rope_done")
        scores_filled = sem("scores_filled")
        scores_read = sem("scores_read")
        shifted = sem("shifted")
        exp_done = sem("exp_done")
        probs_ready = sem("probs_ready")
        probsT_filled = sem("probsT_filled")
        probsT_ready = sem("probsT_ready")
        pv_filled = sem("pv_filled")
        o_copied_act = sem("o_copied_act")
        o_copied_dve = sem("o_copied_dve")
        ld_router = sem("ld_router")
        ld_moe = sem("ld_moe")
        ld_again = sem("ld_again")
        ld_l1 = sem("ld_l1")
        x2s_ready = sem("x2s_ready")
        squares_done = sem("squares_done")
        logits_shifted = sem("logits_shifted")
        logits_exp = sem("logits_exp")
        chosen_ready = sem("chosen_ready")
        tri_ready = sem("tri_ready")
        shared_tanh = sem("shared_tanh")
        shared_ready = sem("shared_ready")
        rows_ready = sem("rows_ready")
        scattered = sem("scattered")
        zeros_ready = sem("zeros_ready")
        map_cleared = sem("map_cleared")
        tok_ready = sem("tok_ready")
        xn_stored = sem("xn_stored")
        blocks_ready = sem("blocks_ready")
        map_gathered = sem("map_gathered")
        tile_tok_ready = sem("tile_tok_ready")
        tables_ready = sem("tables_ready")
        gathered = [sem(f"gathered{n}") for n in range(XB)]
        x_filled = sem("x_filled")
        x_copied = sem("x_copied")
        g_filled = sem("g_filled")
        tanh_done = sem("tanh_done")
        ga_made = sem("ga_made")
        h_made = sem("h_made")
        h_filled = sem("h_filled")
        h_copied = sem("h_copied")
        y_filled = sem("y_filled")
        y_copied = sem("y_copied")
        y_stored = [sem(f"y_stored{n}") for n in range(XB)]
        picked_up = [sem(f"picked_up{n}") for n in range(2)]
        combined = sem("combined")
        z_filled = sem("z_filled")
        z_copied = sem("z_copied")
        hid_filled = sem("hid_filled")
        hid_ready = sem("hid_ready")
        alpha_filled = sem("alpha_filled")
        alpha_shifted = sem("alpha_shifted")
        alpha_exp = sem("alpha_exp")
        vx_filled = sem("vx_filled")
        vx_ready = sem("vx_ready")
        vxT_filled = sem("vxT_filled")
        vxT_ready = sem("vxT_ready")
        o_filled = sem("o_filled")
        final_ready = sem("final_ready")
        stored = sem("stored")

        units = [(c, g) for c in range(NC) for g in range(NPAIR)]
        DVE_JOBS = ("k", "q", "wo", "logits", "shared_gu", "rank", "table", "shared_y")
        jobs = [("cond", c) for c in range(NC)] + [("xT", c) for c in range(NC)]

        def qk_jobs(c, g):
            return [("k", c, g)] + [("q", c, g, j) for j in range(GQ)]

        def v_jobs(c):
            return [("v", c, n) for n in range(CT // 2)]

        jobs += qk_jobs(0, 0) + v_jobs(0) + qk_jobs(0, 1) + qk_jobs(1, 0) + v_jobs(1)
        jobs += [("wo", 0)] + qk_jobs(1, 1) + [("x2T", 0), ("logits", 0), ("shared_gu", 0), ("wo", 1)]
        jobs += [("rank", 0), ("shared_y", 0), ("x2T", 1), ("logits", 1), ("shared_gu", 1), ("rank", 1)]
        jobs += [("table", 0), ("shared_y", 1)]
        place = {job: n for n, job in enumerate(jobs)}
        freed_by = {}
        count = {"act": 0, "dve": 0}
        for job in jobs:
            who = "dve" if job[0] in DVE_JOBS else "act"
            count[who] += 1
            freed_by[job] = (dve_freed if who == "dve" else act_freed, count[who])

        def slot(job):
            n = place[job] % 2
            return ps[:, 2 * n:2 * n + 2, :]

        def wait_filled(eng, job):
            eng.wait_ge(ring_filled, place[job] + 1)

        ropes = [job for job in jobs if job[0] in ("k", "q")]
        rope_no = {job: n for n, job in enumerate(ropes)}
        N_FIRST = 3 + 2 * BT

        def o_dst(g, n, b):
            heads = oT[:, 2 * g * GQ:2 * (g + 1) * GQ, :]
            return heads.rearrange("p j (n i b q) -> p n b i j q", n=2, b=BT, q=S)[:, n, b]

        def o_src(b):
            return ps[:, 4 + b, :].rearrange("p (i j q) -> p i j q", i=2, q=S)

        block = ctx.enter_context(nc.Block())

        @block.sync
        def _(sp):
            sp.dma_start(cst[:], consts).then_inc(ld_first, 16)
            for m, cond in enumerate((cond0, cond1)):
                for q in range(BT):
                    sp.dma_start(cond_sb[S * q:S * q + S, m, :],
                                 cond[q:q + 1, :].broadcast_to([S, NT])).then_inc(ld_first, 16)
            sp.dma_start(x_first, x.rearrange("(i b) c t -> (b c) i t", b=BT)).then_inc(ld_first, 16)
            sp.dma_start(ln1_sb[:], ln1).then_inc(ld_first, 16)
            sp.dma_start(wk_sb[:], wk).then_inc(ld_qkv, 16)
            sp.dma_start(wq_sb[:], wq).then_inc(ld_qkv, 16)
            sp.dma_start(wv_sb[:], wv).then_inc(ld_qkv, 16)
            sp.dma_start(wo_sb[:], wo).then_inc(ld_wo, 16)
            for dst, src in ((gate_sb[:], gate), (bias_sb[:], bias_e.broadcast_to([P, E])),
                             (ln2_sb[:], ln2.broadcast_to([P, H])), (wsg_sb[:], wsg), (wsu_sb[:], wsu), (wsd_sb[:], wsd)):
                sp.dma_start(dst, src).then_inc(ld_router, 16)
            sp.wait_ge(zeros_ready, 1)
            sp.dma_start(token_map.rearrange("(p a n) o -> p a (n o)", p=P, n=P),
                         zeros_i[:, None, :].broadcast_to([P, E * TOK // P // P, P])).then_inc(map_cleared, 16)
            x_rows = xd.rearrange("(i p) t -> p i t", p=P)
            sp.wait_ge(x2s_ready, 1)
            sp.dma_start(x_rows[:, 0:CT, :], xs[:, 0:CT, :]).then_inc(xn_stored, 16)
            sp.wait_ge(rope_done, len(ropes))
            for e0, e1 in ((0, GU_EARLY), (GU_EARLY, E)):
                if e0:
                    sp.wait_ge(scores_filled, 2 * len(units))
                for m, w in enumerate((weg, weu)):
                    sp.dma_start(wgu_sb[:, e0:e1, :, m, :], w[:, e0:e1]).then_inc(ld_moe, 16)
            sp.wait_ge(pv_filled, 2 * len(units))
            sp.dma_start(wed_sb, wed).then_inc(ld_moe, 16)
            sp.wait_ge(x2s_ready, 2)
            sp.dma_start(x_rows[:, CT:NT, :], xs[:, CT:NT, :]).then_inc(xn_stored, 16)
            sp.wait_ge(*freed_by["wo", 1])
            sp.dma_start(x_again, x.rearrange("(i b) c t -> (b c) i t", b=BT)).then_inc(ld_again, 16)
            for dst, src in ((ut_sb, u_t), (vt_sb, v_t), (w1_sb, w1), (b1_sb, b1), (w2_sb, w2),
                             (b2_sb, b2.broadcast_to([P, NSUB]))):
                sp.dma_start(dst, src).then_inc(ld_l1, 16)

            def store_y(n, k):
                sp.wait_ge(y_copied, n + 1)
                sp.dma_start(yd[bass.ds(n * P, P), :], ye[:, k, :]).then_inc(y_stored[k], 16)

            with sp.Fori(0, MOE_TILES // XB) as g:
                for k in range(XB):
                    store_y(g * XB + k, k)
            o_t = out.rearrange("(i b) c t -> i (b c) t", b=BT)
            for i in range(NT):
                sp.wait_ge(final_ready, i + 1)
                sp.dma_start(o_t[i], h_sb[:, i, :]).then_inc(stored, 16)
            sp.wait_ge(stored, 16 * NT)

        @block.gpsimd
        def _(pool):
            pool.wait_ge(cidx_ready, 1)
            for m, w in enumerate((w_cond0, w_cond1)):
                for i in range(NT):
                    pool.indirect_dma_start(out=wst[:, m, i, :], out_offset=None, in_=w,
                                            in_offset=bass.IndirectOffsetOnAxis(ap=cidx[:, m, i:i + 1], axis=0)
                                            ).then_inc(wst_loaded[m], 16)
            pool.wait_ge(k_zeroed, 1)
            for n, job in enumerate(ropes):
                kind, c, g = job[:3]
                u = units.index((c, g))
                pool.wait_ge(rope_prod, n + 1)
                if u >= 2:
                    pool.wait_ge(scores_filled, 2 * (u - 1))
                a = rope_c[:, n % 2].rearrange("p e (b s) -> p e b s", s=S)
                b = rope_s[:, n % 2].rearrange("p e (b s) -> p e b s", s=S)
                if kind == "k":
                    for s in range(2):
                        lanes = slice(FR * s, FR * s + FR)
                        last = nc.gpsimd.tensor_tensor(k_sb[lanes, u % 2, :, :, s, :], a[lanes], b[lanes], ALU.add)
                else:
                    last = nc.gpsimd.tensor_tensor(q_sb[:, u % 2, :, :, job[3], :], a, b, ALU.add)
                last.then_inc(rope_done, 1)
                if kind == "k":
                    pool.wait_ge(rope_done, n + 1)

            pool.wait_ge(map_cleared, 16)
            pool.wait_ge(tok_ready, 1)
            for c in range(NC):
                pool.wait_ge(rows_ready, c + 1)
                for i in range(c * CT, (c + 1) * CT):
                    for k in range(K):
                        pool.indirect_dma_start(out=token_map, out_offset=bass.IndirectOffsetOnAxis(ap=row_i[:, i, k:k + 1], axis=0),
                                                in_=tok_i[:, i:i + 1], in_offset=None).then_inc(scattered, 16)
            pool.wait_ge(blocks_ready, 1)
            pool.wait_ge(scattered, 16 * NT * K)
            pool.indirect_dma_start(out=tile_tok_i[0:MOE_TILES, :], out_offset=None,
                                    in_=token_map.rearrange("(a n) o -> a (n o)", n=P),
                                    in_offset=bass.IndirectOffsetOnAxis(ap=block_i[0:MOE_TILES, :], axis=0)).then_inc(map_gathered, 16)
            pool.wait_ge(tables_ready, 1)
            pool.wait_ge(xn_stored, 32)

            for n in range(MOE_TILES):
                if n >= XB:
                    pool.wait_ge(x_filled, n - XB + 1)
                pool.indirect_dma_start(out=xg[:, n % XB, :], out_offset=None, in_=xd,
                                        in_offset=bass.IndirectOffsetOnAxis(ap=src_i[:, n:n + 1], axis=0)
                                        ).then_inc(gathered[n % XB], 16)
            for k in range(XB):
                pool.wait_ge(y_stored[k], 16 * (MOE_TILES // XB))
            for i in range(NT):
                if i >= 2:
                    pool.wait_ge(combined, i - 1)
                for k in range(K):
                    pool.indirect_dma_start(out=yg[:, i % 2, k, :], out_offset=None, in_=yd,
                                            in_offset=bass.IndirectOffsetOnAxis(ap=slot_i[:, i, k:k + 1], axis=0)
                                            ).then_inc(picked_up[i % 2], 16)

        @block.scalar
        def _(act):
            for c in range(NC):
                wait_filled(act, ("cond", c))
                y = slot(("cond", c)).rearrange("p b (i t) -> p (b i) t", t=H)
                for i in range(CT):
                    nc.scalar.activation(xs[:, c * CT + i, :], y[:, i, :], ACT.Square,
                                         accum_out=ss[:, c * CT + i:c * CT + i + 1])
                nc.scalar.activation(h_sb[:, c * CT:(c + 1) * CT, :], y, ACT.Copy).then_inc(act_freed, 1)
            for c in range(NC):
                wait_filled(act, ("xT", c))
                if c == 0:
                    act.wait_ge(ld_first, 16 * N_FIRST)
                for hc in range(HC):
                    last = nc.scalar.activation(xT[:, hc, c * CW:(c + 1) * CW], slot(("xT", c))[:, hc, :], ACT.Copy,
                                                scale=ln1_sb[:, hc:hc + 1])
                last.then_inc(act_freed, 1)

            def copy_v(c):
                for n in range(CT // 2):
                    wait_filled(act, ("v", c, n))
                    nc.scalar.activation(v_sb[:, 2 * n:2 * n + 2, :], slot(("v", c, n)), ACT.Copy).then_inc(act_freed, 1)

            def exps(u):
                for s in range(2):
                    act.wait_ge(shifted, 2 * u + s + 1)
                    nc.scalar.activation(pr[:, s], pr[:, s], ACT.Exp, scale=SM_SCALE).then_inc(exp_done, 1)

            def copy_probsT(u):
                for s in range(2):
                    act.wait_ge(probsT_filled, 2 * u + s + 1)
                    nc.scalar.activation(prT[:, s], ps[:, 6 + s, :].rearrange("p (i k t) -> p i k t", i=2, k=2),
                                         ACT.Copy).then_inc(probsT_ready, 1)

            def copy_o(u):
                c, g = units[u]
                for n in range(2):
                    act.wait_ge(pv_filled, 2 * u + n + 1)
                    for b in range(2):
                        last = nc.scalar.activation(o_dst(g, n, b), o_src(b), ACT.Copy)
                    last.then_inc(o_copied_act, 1)

            copy_v(0)
            exps(0)
            copy_probsT(0)
            copy_o(0)
            exps(1)
            copy_probsT(1)
            copy_o(1)
            copy_v(1)
            exps(2)

            def squares(c):
                act.wait_ge(dve_freed, freed_by["wo", c][1])
                for i in range(c * CT, (c + 1) * CT):
                    last = nc.scalar.activation(xs[:, i, :], h_sb[:, i, :], ACT.Square, accum_out=ss[:, i:i + 1])
                last.then_inc(squares_done, 1)

            def router(c):
                wait_filled(act, ("x2T", c))
                nc.scalar.activation(xT[:, :, c * CW:(c + 1) * CW], slot(("x2T", c)), ACT.Copy).then_inc(act_freed, 1)
                act.wait_ge(logits_shifted, c + 1)
                p = probs[:, c * CT:(c + 1) * CT, :]
                nc.scalar.activation(p, p, ACT.Exp).then_inc(logits_exp, 1)
                wait_filled(act, ("shared_gu", c))
                if c:
                    act.wait_ge(ring_filled, place["shared_y", c - 1] + 1)
                nc.scalar.activation(sh[:], slot(("shared_gu", c))[:, 0, :], ACT.Tanh, scale=0.5).then_inc(shared_tanh, 1)

            squares(0)
            copy_probsT(2)
            copy_o(2)
            exps(3)
            router(0)
            copy_probsT(3)
            copy_o(3)
            squares(1)
            router(1)

            def copy_x(n, k, first):
                act.wait_ge(x_filled, n + 1)
                if not first:
                    act.wait_ge(g_filled, n - 1)
                nc.scalar.activation(xgT[:, k % 2], ps[:, k % 2, 0:H].rearrange("p (c t) -> p c t", c=HC),
                                     ACT.Copy).then_inc(x_copied, 1)

            def tanh(n, k, first):
                act.wait_ge(g_filled, n + 1)
                if not first:
                    act.wait_ge(h_made, n - 1)
                nc.scalar.activation(th[:, k % 2], ps[:, 2 + k % 2, 0:I], ACT.Tanh, scale=0.5).then_inc(tanh_done, 1)

            def copy_y(n, k, first):
                act.wait_ge(y_filled, n + 1)
                if not first:
                    act.wait_ge(y_stored[k], (n - k) * (16 // XB))
                nc.scalar.activation(ye[:, k, :], ps[:, 6 + k % 2, 0:H], ACT.Copy).then_inc(y_copied, 1)

            copy_x(0, 0, True)
            copy_x(1, 1, True)
            tanh(0, 0, True)
            copy_x(2, 2, False)
            tanh(1, 1, True)
            copy_x(3, 3, False)
            tanh(2, 2, False)
            copy_y(0, 0, True)
            for k in range(XB - 1):
                copy_x(XB + k, k, False)
                tanh(XB + k - 1, (k - 1) % XB, False)
                copy_y(k + 1, k + 1, True)
            with act.Fori(1, MOE_TILES // XB - 1) as g:
                for k in range(XB):
                    n = g * XB + XB - 1 + k
                    copy_x(n, (k - 1) % XB, False)
                    tanh(n - 1, (k - 2) % XB, False)
                    copy_y(n - 3, k, False)
            n = MOE_TILES - 1
            copy_x(n, 3, False)
            tanh(n - 1, 2, False)
            copy_y(n - 3, 0, False)
            tanh(n, 3, False)
            copy_y(n - 2, 1, False)
            copy_y(n - 1, 2, False)
            copy_y(n, 3, False)

            act.wait_ge(ld_l1, 16 * 6)
            for i in range(NT):
                act.wait_ge(z_filled, i + 1)
                nc.scalar.activation(zT[:, i % 2], ps[:, 0, 0:H].rearrange("p (c t) -> p c t", c=HC), ACT.Copy).then_inc(z_copied, 1)
                if i:
                    act.wait_ge(vxT_filled, i)
                    nc.scalar.activation(vxT[:, (i - 1) % 2], ps[:, 5, :].rearrange("p (m t) -> p m t", t=P),
                                         ACT.Copy).then_inc(vxT_ready, 1)
                act.wait_ge(hid_filled, i + 1)
                for hc in range(HC):
                    last = nc.scalar.activation(hT[:, i % 2, hc], ps[:, 1, hc * P:(hc + 1) * P], ACT.Relu, bias=b1_sb[:, hc:hc + 1])
                last.then_inc(hid_ready, 1)
                act.wait_ge(alpha_shifted, i + 1)
                nc.scalar.activation(al[:, i % 2, 1], al[:, i % 2, 0], ACT.Exp, accum_out=al[:, i % 2, 3, 1:2]).then_inc(alpha_exp, 1)
            act.wait_ge(vxT_filled, NT)
            nc.scalar.activation(vxT[:, (NT - 1) % 2], ps[:, 5, :].rearrange("p (m t) -> p m t", t=P), ACT.Copy).then_inc(vxT_ready, 1)

        @block.vector
        def _(dve):
            step = [0]

            def link(ins):
                step[0] += 1
                ins.then_inc(dve_step, 1)
                dve.wait_ge(dve_step, step[0])

            def rsqrt_mean(c, v, y, t):
                link(nc.vector.tensor_scalar(v, ss[:, c * CT:(c + 1) * CT], 1.0 / H, EPS, ALU.mult, ALU.add))
                link(nc.vector.tensor_scalar(y.bitcast(I32), v.bitcast(I32), -0.5, RSQRT_SEED, ALU.mult, ALU.add))
                for _ in range(3):
                    link(nc.vector.scalar_tensor_tensor(out=t, in0=y, scalar=-0.5, in1=y, op0=ALU.mult, op1=ALU.mult))
                    link(nc.vector.tensor_tensor(t, t, v, ALU.mult))
                    link(nc.vector.scalar_tensor_tensor(out=y, in0=t, scalar=1.5, in1=y, op0=ALU.add, op1=ALU.mult))

            nc.vector.memset(wbd[:], 0.0)
            nc.vector.memset(k_sb[:], 0.0).then_inc(k_zeroed, 1)
            dve.wait_ge(ld_first, 16 * N_FIRST)
            nc.vector.tensor_scalar(cidx[:], cond_sb[:], float(S), cst[:, C_PMOD:C_PMOD + 1],
                                    ALU.mult, ALU.add).then_inc(cidx_ready, 1)
            for m in range(2):
                dve.wait_ge(wst_loaded[m], 16 * NT)
                for q in range(BT):
                    last = nc.vector.tensor_copy(wbd[S * q:S * q + S, m, :, S * q:S * q + S], wst[S * q:S * q + S, m])
                last.then_inc(wbd_ready, 1)
                if m == 0:
                    for c in range(NC):
                        dve.wait_ge(act_freed, freed_by["cond", c][1])
                        v, y, t = rs[:, 0], rs[:, 1], rs[:, 2]
                        rsqrt_mean(c, v, y, t)
                        for i in range(CT):
                            n = c * CT + i
                            last = nc.vector.tensor_scalar(xs[:, n, :], h_sb[:, n, :], y[:, i:i + 1], None, ALU.mult)
                        last.then_inc(xs_ready, 1)

            def rope(job):
                n = rope_no[job]
                wait_filled(dve, job)
                if n >= 2:
                    dve.wait_ge(rope_done, n - 1)
                y = slot(job).rearrange("p e (b s) -> p e b s", s=S)
                shape = [P, 2, CW // S, S]
                nc.vector.tensor_tensor(rope_c[:, n % 2].rearrange("p e (b s) -> p e b s", s=S), y,
                                        cosT[:, None, None, :].broadcast_to(shape), ALU.mult)
                ins = nc.vector.tensor_tensor(rope_s[:, n % 2].rearrange("p e (b s) -> p e b s", s=S), y[:, ::-1],
                                              sinT[:, :, None, :].broadcast_to(shape), ALU.mult)
                ins.then_inc(dve_freed, 1)
                dve.wait_ge(dve_freed, freed_by[job][1])
                dve.sem_inc(rope_prod, 1)

            def rows_of(n):
                return pr[:, n].rearrange("p i s b k -> p (i s b) k")

            def softmax_shift(u):
                for n in range(2):
                    dve.wait_ge(scores_filled, 2 * u + n + 1)
                    link(nc.vector.tensor_tensor(rows_of(n), ps[:, 4 + n, :].rearrange("p (n t) -> p n t", t=S),
                                                 mask[:, None, :].broadcast_to([P, CT * BT, S]), ALU.add))
                    link(nc.vector.tensor_reduce(st[:, n, 0], rows_of(n), AX, ALU.max))
                    nc.vector.tensor_tensor(rows_of(n), rows_of(n), st[:, n, 0, :, None].broadcast_to([P, CT * BT, S]),
                                            ALU.subtract).then_inc(shifted, 1)

            def softmax_norm(u):
                for n in range(2):
                    dve.wait_ge(exp_done, 2 * u + n + 1)
                    link(nc.vector.tensor_reduce(st[:, n, 1], rows_of(n), AX, ALU.add))
                    link(nc.vector.reciprocal(st[:, n, 2], st[:, n, 1]))
                    nc.vector.tensor_tensor(rows_of(n), rows_of(n), st[:, n, 2, :, None].broadcast_to([P, CT * BT, S]),
                                            ALU.mult).then_inc(probs_ready, 1)

            def copy_o(u):
                c, g = units[u]
                for n in range(2):
                    dve.wait_ge(pv_filled, 2 * u + n + 1)
                    for b in range(2, BT):
                        last = nc.vector.tensor_copy(o_dst(g, n, b), o_src(b))
                    last.then_inc(o_copied_dve, 1)

            def residual(c):
                wait_filled(dve, ("wo", c))
                hc = h_sb[:, c * CT:(c + 1) * CT, :]
                y = slot(("wo", c)).rearrange("p b (i t) -> p (b i) t", t=H)
                nc.vector.tensor_tensor(hc, y, hc, ALU.add).then_inc(dve_freed, 1)

            def second_norm(c):
                dve.wait_ge(squares_done, c + 1)
                if c == 0:
                    dve.wait_ge(ld_router, 16 * 6)
                v, y, t = rs[:, 0], rs[:, 1], rs[:, 2]
                rsqrt_mean(c, v, y, t)
                for i in range(CT):
                    n = c * CT + i
                    last = nc.vector.scalar_tensor_tensor(out=xs[:, n, :], in0=h_sb[:, n, :], scalar=y[:, i:i + 1],
                                                          in1=ln2_sb[:], op0=ALU.mult, op1=ALU.mult)
                last.then_inc(x2s_ready, 1)

            def router_shift(c):
                wait_filled(dve, ("logits", c))
                y = slot(("logits", c))[:, 0, 0:CT * E].rearrange("p (i e) -> p i e", e=E)
                link(nc.vector.tensor_reduce(rt[:, 0], y, AX, ALU.max))
                ins = nc.vector.tensor_tensor(probs[:, c * CT:(c + 1) * CT, :], y,
                                              rt[:, 0, :, None].broadcast_to([P, CT, E]), ALU.subtract)
                ins.then_inc(dve_freed, 1)
                dve.wait_ge(dve_freed, freed_by["logits", c][1])
                dve.sem_inc(logits_shifted, 1)

            def router_choose(c):
                tiles = slice(c * CT, (c + 1) * CT)
                p = probs[:, tiles, :]
                dve.wait_ge(logits_exp, c + 1)
                link(nc.vector.tensor_reduce(rt[:, 1], p, AX, ALU.add))
                link(nc.vector.reciprocal(rt[:, 2], rt[:, 1]))
                link(nc.vector.tensor_tensor(p, p, rt[:, 2, :, None].broadcast_to([P, CT, E]), ALU.mult))
                link(nc.vector.tensor_tensor(biased[:, tiles, :], p, bias_sb[:, None, :].broadcast_to([P, CT, E]), ALU.add))
                for i in range(c * CT, (c + 1) * CT):
                    last = nc.vector.max(top[:, i, :], biased[:, i, :])
                link(last)
                for i in range(c * CT, (c + 1) * CT):
                    last = nc.vector.max_index(top_at[:, i, :], top[:, i, :], biased[:, i, :])
                link(last)
                link(nc.vector.tensor_copy(top_f[:, tiles, :], top_at[:, tiles, 0:K]))
                flags = picked[:, tiles].rearrange("p i k e -> p (i k) e")
                link(nc.vector.tensor_tensor(flags, cst[:, None, C_IOTA:C_ROW0].broadcast_to([P, CT * K, E]),
                                             top_f[:, tiles, :].rearrange("p i k -> p (i k)")[:, :, None].broadcast_to([P, CT * K, E]),
                                             ALU.is_equal))
                with nc.allow_low_precision(reason="sums of flags are 0 or 1"):
                    nc.vector.tensor_reduce(chosen[:, tiles, :], picked[:, tiles].rearrange("p i k e -> p i e k"),
                                            AX, ALU.add).then_inc(chosen_ready, 1)
                link(nc.vector.tensor_tensor(tmp_ke[:], picked[:, tiles], p[:, :, None, :].broadcast_to([P, CT, K, E]), ALU.mult))
                link(nc.vector.tensor_reduce(w4[:, tiles, :], tmp_ke[:], AX, ALU.add))
                link(nc.vector.tensor_reduce(rw[:, 0, tiles], w4[:, tiles, :], AX, ALU.add))
                link(nc.vector.tensor_scalar(rw[:, 0, tiles], rw[:, 0, tiles], NORM_MIN, None, ALU.max))
                link(nc.vector.reciprocal(rw[:, 1, tiles], rw[:, 0, tiles]))
                link(nc.vector.tensor_scalar(rw[:, 1, tiles], rw[:, 1, tiles], 0.5, None, ALU.mult))
                link(nc.vector.tensor_tensor(w4[:, tiles, :], w4[:, tiles, :],
                                             rw[:, 1, tiles, None].broadcast_to([P, CT, K]), ALU.mult))

            def shared_hidden(c):
                dve.wait_ge(shared_tanh, c + 1)
                y = slot(("shared_gu", c))
                link(nc.vector.scalar_tensor_tensor(out=sh[:], in0=sh[:], scalar=1.0, in1=y[:, 0, :], op0=ALU.add, op1=ALU.mult))
                nc.vector.scalar_tensor_tensor(out=sh[:], in0=sh[:], scalar=0.5, in1=y[:, 1, :],
                                               op0=ALU.mult, op1=ALU.mult).then_inc(dve_freed, 1)

            def rows(c):
                tiles = slice(c * CT, (c + 1) * CT)
                wait_filled(dve, ("rank", c))
                y = slot(("rank", c))[:, 0, 0:CT * E].rearrange("p (i e) -> p i e", e=E)
                link(nc.vector.tensor_copy(rank[:, tiles, :], y))
                link(nc.vector.tensor_tensor(row_of[:, tiles, :], rank[:, tiles, :],
                                             cst[:, None, C_ROW0:C_PART].broadcast_to([P, CT, E]), ALU.add))
                link(nc.vector.tensor_tensor(tmp_ke[:], picked[:, tiles], row_of[:, tiles, None, :].broadcast_to([P, CT, K, E]), ALU.mult))
                link(nc.vector.tensor_reduce(row_f[:, tiles, :], tmp_ke[:], AX, ALU.add))
                nc.vector.tensor_copy(row_i[:, tiles, :], row_f[:, tiles, :]).then_inc(rows_ready, 1)
                if c == 0:
                    dve.sem_inc(dve_freed, 1)

            def tile_tables():
                n_e, c_e, cum, first, done, t = (tab[:, m] for m in range(6))
                link(nc.vector.tensor_copy(n_e, slot(("rank", 1))[:, 1, 0:E]))
                dve.sem_inc(dve_freed, 1)
                link(nc.vector.tensor_scalar(tab_i[:, 0], n_e, float(P - 1), None, ALU.add))
                link(nc.vector.tensor_scalar(tab_i[:, 1], tab_i[:, 0], 7, None, ALU.logical_shift_right))
                link(nc.vector.tensor_copy(c_e, tab_i[:, 1]))
                link(nc.vector.memset(t, 0.0))
                link(nc.vector.tensor_tensor_scan(cum, c_e, t, 0.0, ALU.add, ALU.add))
                link(nc.vector.tensor_tensor(first, cum, c_e, ALU.subtract))
                tile, mine, before, block = (col[:, m:m + 1] for m in range(4))
                link(nc.vector.tensor_scalar(tile, cum[:, E - 1:E], -1.0, cst[:, C_PART:C_PART + 1], ALU.add, ALU.min))
                link(nc.vector.tensor_scalar(done, cum, tile, None, ALU.is_le))
                link(nc.vector.tensor_reduce(mine, done, AX, ALU.add))
                link(nc.vector.tensor_tensor(t, done, c_e, ALU.mult))
                link(nc.vector.tensor_reduce(before, t, AX, ALU.add))
                link(nc.vector.tensor_tensor(block, tile, before, ALU.subtract))
                nc.vector.scalar_tensor_tensor(out=block_i[:], in0=mine, scalar=float(TOK // P), in1=block,
                                               op0=ALU.mult, op1=ALU.add).then_inc(blocks_ready, 1)
                link(nc.vector.tensor_scalar(first, first, float(P), None, ALU.mult))
                link(nc.vector.tensor_tensor(row_of[:], rank[:], first[:, None, :].broadcast_to([P, NT, E]), ALU.add))
                for c in range(NC):
                    tiles = slice(c * CT, (c + 1) * CT)
                    link(nc.vector.tensor_tensor(tmp_ke[:], picked[:, tiles],
                                                 row_of[:, tiles, None, :].broadcast_to([P, CT, K, E]), ALU.mult))
                    link(nc.vector.tensor_reduce(slot_f[:, tiles, :], tmp_ke[:], AX, ALU.add))
                nc.vector.tensor_copy(slot_i[:], slot_f[:])
                M = MOE_TILES
                dve.wait_ge(map_gathered, 16)
                nc.vector.tensor_copy(tile_tok[0:M], tile_tok_i[0:M]).then_inc(tile_tok_ready, 1)
                wait_filled(dve, ("table", 0))
                y = slot(("table", 0))[:, 0, :]
                link(nc.vector.tensor_copy(expert_of[:], y[0:1, M:2 * M]))
                nc.vector.tensor_copy(src_i[:], y[:, 0:M]).then_inc(dve_freed, 1)
                dve.wait_ge(dve_freed, freed_by["table", 0][1])
                dve.sem_inc(tables_ready, 1)

            def shared_add(c):
                wait_filled(dve, ("shared_y", c))
                hc = h_sb[:, c * CT:(c + 1) * CT, :]
                ins = nc.vector.tensor_tensor(hc, slot(("shared_y", c)).rearrange("p b (i t) -> p (b i) t", t=H), hc, ALU.add)
                ins.then_inc(dve_freed, 1)
                dve.wait_ge(dve_freed, freed_by["shared_y", c][1])
                if c == 0:
                    dve.wait_ge(ld_again, 16)
                link(nc.vector.tensor_tensor(hc, hc, x_again[:, c * CT:(c + 1) * CT, :], ALU.add))

            nc.vector.memset(ones[:], 1.0)
            nc.vector.memset(zeros_i[:], 0).then_inc(zeros_ready, 1)
            nc.vector.tensor_copy(tok_i[:], cst[:, C_TOK:C_END]).then_inc(tok_ready, 1)
            nc.vector.tensor_copy(tri[:], cst[:, C_TRI:C_IOTA]).then_inc(tri_ready, 1)
            for job in qk_jobs(0, 0):
                rope(job)
            softmax_shift(0)
            for n, job in enumerate(qk_jobs(0, 1)):
                rope(job)
                if n == 1:
                    softmax_norm(0)
            copy_o(0)
            softmax_shift(1)
            for n, job in enumerate(qk_jobs(1, 0)):
                rope(job)
                if n == 1:
                    softmax_norm(1)
            copy_o(1)
            softmax_shift(2)
            residual(0)
            for n, job in enumerate(qk_jobs(1, 1)):
                rope(job)
                if n == 1:
                    softmax_norm(2)
                if n == 2:
                    second_norm(0)
            copy_o(2)
            softmax_shift(3)
            router_shift(0)
            softmax_norm(3)
            shared_hidden(0)
            router_choose(0)
            copy_o(3)
            residual(1)
            second_norm(1)
            rows(0)
            shared_add(0)
            router_shift(1)
            router_choose(1)
            shared_hidden(1)
            rows(1)
            tile_tables()
            shared_add(1)

            def hidden(n, k, first):
                dve.wait_ge(tanh_done, n + 1)
                g, u = ps[:, 2 + k % 2, 0:I], ps[:, 2 + k % 2, I:2 * I]
                nc.vector.scalar_tensor_tensor(out=ga[:, k % 2], in0=th[:, k % 2], scalar=1.0, in1=g,
                                               op0=ALU.add, op1=ALU.mult).then_inc(ga_made, 1)
                dve.wait_ge(ga_made, n + 1)
                if not first:
                    dve.wait_ge(h_filled, n - 1)
                nc.vector.tensor_tensor(hm[:, k % 2], ga[:, k % 2], u, ALU.mult).then_inc(h_made, 1)

            def copy_h(n, k, first):
                dve.wait_ge(h_filled, n + 1)
                if not first:
                    dve.wait_ge(y_filled, n - 1)
                nc.vector.tensor_copy(hmT[:, k % 2], ps[:, 4 + k % 2, 0:P]).then_inc(h_copied, 1)

            hidden(0, 0, True)
            hidden(1, 1, True)
            copy_h(0, 0, True)
            hidden(2, 2, False)
            copy_h(1, 1, True)
            for k in range(XB):
                hidden(XB - 1 + k, (k - 1) % XB, False)
                copy_h(XB - 2 + k, (k - 2) % XB, False)
            with dve.Fori(1, MOE_TILES // XB - 1) as g:
                for k in range(XB):
                    n = g * XB + XB - 1 + k
                    hidden(n, (k - 1) % XB, False)
                    copy_h(n - 1, (k - 2) % XB, False)
            hidden(MOE_TILES - 1, 3, False)
            copy_h(MOE_TILES - 2, 2, False)
            copy_h(MOE_TILES - 1, 3, False)

            def combine(i):
                dve.wait_ge(picked_up[i % 2], 16 * K * (i // 2 + 1))
                for k in range(K):
                    ins = nc.vector.scalar_tensor_tensor(out=h_sb[:, i, :], in0=yg[:, i % 2, k, :], scalar=w4[:, i, k:k + 1],
                                                         in1=h_sb[:, i, :], op0=ALU.mult, op1=ALU.add)
                    if k < K - 1:
                        link(ins)
                ins.then_inc(combined, 1)

            def finish(i):
                dve.wait_ge(o_filled, i + 1)
                nc.vector.tensor_tensor(h_sb[:, i, :], ps[:, 6 + i % 2, 0:H], h_sb[:, i, :], ALU.add).then_inc(final_ready, 1)

            combine(0)
            for i in range(NT):
                a = al[:, i % 2]
                if i + 1 < NT:
                    combine(i + 1)
                dve.wait_ge(alpha_filled, i + 1)
                if i == 0:
                    dve.wait_ge(ld_l1, 16 * 6)
                link(nc.vector.tensor_tensor(a[:, 0], ps[:, 4, 0:NSUB], b2_sb[:], ALU.add))
                link(nc.vector.tensor_reduce(a[:, 3, 0:1], a[:, 0], AX, ALU.max))
                nc.vector.tensor_scalar(a[:, 0], a[:, 0], a[:, 3, 0:1], None, ALU.subtract).then_inc(alpha_shifted, 1)
                dve.wait_ge(alpha_exp, i + 1)
                link(nc.vector.reciprocal(a[:, 3, 2:3], a[:, 3, 1:2]))
                link(nc.vector.tensor_scalar(a[:, 2], a[:, 1], a[:, 3, 2:3], None, ALU.mult))
                dve.wait_ge(vx_filled, i + 1)
                nc.vector.tensor_tensor(vx[:, i % 2].rearrange("p (k r) -> p k r", r=R),
                                        ps[:, 2 + i % 2, :].rearrange("p (k r) -> p k r", r=R),
                                        a[:, 2, :, None].broadcast_to([P, NSUB, R]), ALU.mult).then_inc(vx_ready, 1)
                if i:
                    finish(i - 1)
            finish(NT - 1)

        @block.tensor
        def _(pe):
            def claim(job):
                n = place[job]
                if n >= 2:
                    pe.wait_ge(*freed_by[jobs[n - 2]])

            pe.wait_ge(wbd_ready, 1)
            pe.wait_ge(ld_first, 16 * N_FIRST)
            for c in range(NC):
                claim(("cond", c))
                y = slot(("cond", c)).rearrange("p b (i t) -> p (b i) t", t=H)
                for i in range(CT):
                    last = nc.tensor.matmul(y[:, i, :], wbd[:, 0, c * CT + i, :], x_first[:, c * CT + i, :], start=True, stop=True)
                last.then_inc(ring_filled, 1)
            for c in range(NC):
                claim(("xT", c))
                pe.wait_ge(xs_ready, c + 1)
                for i in range(CT):
                    for hc in range(HC):
                        last = nc.tensor.transpose(slot(("xT", c))[:, hc, i * P:(i + 1) * P],
                                                   xs[:, c * CT + i, hc * P:(hc + 1) * P], ident)
                last.then_inc(ring_filled, 1)

            def project_qk(c, g):
                pe.wait_ge(act_freed, freed_by["xT", c][1])
                for job in qk_jobs(c, g):
                    claim(job)
                    for e in range(2):
                        for hc in range(HC):
                            w = wk_sb[:, hc, g, e, :] if job[0] == "k" else wq_sb[:, hc, g, job[3], e, :]
                            last = nc.tensor.matmul(slot(job)[:, e, :], w, xT[:, hc, c * CW:(c + 1) * CW],
                                                    start=(hc == 0), stop=(hc == HC - 1))
                    last.then_inc(ring_filled, 1)

            def project_v(c):
                for job in v_jobs(c):
                    claim(job)
                    for n in range(2):
                        i = c * CT + 2 * job[2] + n
                        for hc in range(HC):
                            last = nc.tensor.matmul(slot(job)[:, n, :], xT[:, hc, i * P:(i + 1) * P], wv_sb[:, hc, :],
                                                    start=(hc == 0), stop=(hc == HC - 1))
                    last.then_inc(ring_filled, 1)

            def scores(u):
                pe.wait_ge(rope_done, (u + 1) * (GQ + 1))
                if u:
                    pe.wait_ge(o_copied_act, 2 * u)
                for n in range(2):
                    bank = ps[:, 4 + n, :].rearrange("p (i s b k) -> p i b s k", i=2, s=2, b=BT)
                    for i in range(2):
                        for b in range(BT):
                            blk = (2 * n + i) * BT + b
                            for e in range(2):
                                last = nc.tensor.matmul(bank[:, i, b], q_sb[:, u % 2, e, blk].rearrange("p j q -> p (j q)"),
                                                        k_sb[:, u % 2, e, blk].rearrange("p s k -> p (s k)"),
                                                        start=(e == 0), stop=(e == 1))
                    last.then_inc(scores_filled, 1)

            def attend(u):
                c, g = units[u]
                for n in range(2):
                    pe.wait_ge(probs_ready, 2 * u + n + 1)
                    if u and n == 0:
                        pe.wait_ge(o_copied_dve, 2 * u)
                    for i in range(2):
                        for s in range(2):
                            last = nc.tensor.transpose(ps[:, 6 + n, (2 * i + s) * P:(2 * i + s + 1) * P],
                                                       pr[:, n, i, s].rearrange("p b k -> p (b k)"), ident)
                    last.then_inc(probsT_filled, 1)
                for n in range(2):
                    if n == 0:
                        pe.wait_ge(probsT_ready, 2 * u + 2)
                        pe.wait_ge(act_freed, freed_by["v", c, CT // 2 - 1][1])
                    else:
                        pe.wait_ge(o_copied_act, 2 * u + 1)
                        pe.wait_ge(o_copied_dve, 2 * u + 1)
                    for i in range(2):
                        for s in range(2):
                            kv = 2 * g + s
                            for b in range(BT):
                                rows = slice(S * b, S * b + S)
                                last = nc.tensor.matmul(ps[:, 4 + b, (2 * i + s) * P:(2 * i + s + 1) * P],
                                                        v_sb[rows, 2 * n + i, kv * D:(kv + 1) * D],
                                                        prT[rows, n, i, s, :], start=True, stop=True)
                    last.then_inc(pv_filled, 1)

            def project_o(c):
                claim(("wo", c))
                pe.wait_ge(o_copied_act, 4 * (c + 1))
                pe.wait_ge(o_copied_dve, 4 * (c + 1))
                if c == 0:
                    pe.wait_ge(ld_wo, 16)
                y = slot(("wo", c)).rearrange("p b (i t) -> p (b i) t", t=H)
                for i in range(CT):
                    for h in range(HQ):
                        last = nc.tensor.matmul(y[:, i, :], oT[:, h, i * P:(i + 1) * P], wo_sb[:, h, :],
                                                start=(h == 0), stop=(h == HQ - 1))
                last.then_inc(ring_filled, 1)

            pe.wait_ge(ld_qkv, 48)
            project_qk(0, 0)
            project_v(0)
            scores(0)
            project_qk(0, 1)
            attend(0)
            scores(1)
            project_qk(1, 0)
            project_v(1)
            attend(1)
            scores(2)
            project_o(0)
            project_qk(1, 1)
            attend(2)
            scores(3)
            def transpose_second(c):
                claim(("x2T", c))
                pe.wait_ge(x2s_ready, c + 1)
                for i in range(CT):
                    for hc in range(HC):
                        last = nc.tensor.transpose(slot(("x2T", c))[:, hc, i * P:(i + 1) * P],
                                                   xs[:, c * CT + i, hc * P:(hc + 1) * P], ident)
                last.then_inc(ring_filled, 1)

            def router(c):
                pe.wait_ge(act_freed, freed_by["x2T", c][1])
                if c == 0:
                    pe.wait_ge(ld_router, 16 * 6)
                claim(("logits", c))
                for i in range(CT):
                    n = c * CT + i
                    for hc in range(HC):
                        last = nc.tensor.matmul(slot(("logits", c))[:, 0, i * E:(i + 1) * E], xT[:, hc, n * P:(n + 1) * P],
                                                gate_sb[:, hc, :], start=(hc == 0), stop=(hc == HC - 1))
                last.then_inc(ring_filled, 1)
                claim(("shared_gu", c))
                for m, w in enumerate((wsg_sb, wsu_sb)):
                    for hc in range(HC):
                        last = nc.tensor.matmul(slot(("shared_gu", c))[:, m, :], w[:, hc, :], xT[:, hc, c * CW:(c + 1) * CW],
                                                start=(hc == 0), stop=(hc == HC - 1))
                last.then_inc(ring_filled, 1)

            def ranks(c):
                claim(("rank", c))
                pe.wait_ge(chosen_ready, c + 1)
                if c == 0:
                    pe.wait_ge(tri_ready, 1)
                for i in range(CT):
                    n = c * CT + i
                    y = slot(("rank", c))[:, 0, i * E:(i + 1) * E]
                    last = nc.tensor.matmul(y, tri[:], chosen[:, n, :], start=True, stop=(n == 0))
                    for m in range(n):
                        last = nc.tensor.matmul(y, ones[:], chosen[:, m, :], start=False, stop=(m == n - 1))
                if c == NC - 1:
                    for m in range(NT):
                        last = nc.tensor.matmul(slot(("rank", c))[:, 1, 0:E], ones[:], chosen[:, m, :],
                                                start=(m == 0), stop=(m == NT - 1))
                last.then_inc(ring_filled, 1)

            def shared_out(c):
                claim(("shared_y", c))
                pe.wait_ge(*freed_by["shared_gu", c])
                y = slot(("shared_y", c)).rearrange("p b (i t) -> p (b i) t", t=H)
                for i in range(CT):
                    last = nc.tensor.matmul(y[:, i, :], sh[:, i * P:(i + 1) * P], wsd_sb[:], start=True, stop=True)
                last.then_inc(ring_filled, 1)

            transpose_second(0)
            router(0)
            attend(3)
            project_o(1)
            ranks(0)
            shared_out(0)
            transpose_second(1)
            router(1)
            ranks(1)
            claim(("table", 0))
            pe.wait_ge(tile_tok_ready, 1)
            M = MOE_TILES
            nc.tensor.transpose(slot(("table", 0))[:, 0, 0:M], tile_tok[0:M], ident[0:M, 0:M])
            nc.tensor.transpose(slot(("table", 0))[0:1, 0, M:2 * M], col[0:M, 1:2], ident[0:M, 0:M]).then_inc(ring_filled, 1)
            shared_out(1)

            pe.wait_ge(ld_moe, 16 * 5)
            pe.wait_ge(*freed_by["shared_y", 1])
            pe.wait_ge(tables_ready, 1)

            def transpose_x(n, k, first):
                pe.wait_ge(gathered[k], (n - k) * (16 // XB) + 16)
                if not first:
                    pe.wait_ge(x_copied, n - 1)
                for hc in range(HC):
                    last = nc.tensor.transpose(ps[:, k % 2, hc * P:(hc + 1) * P], xg[:, k, hc * P:(hc + 1) * P], ident)
                last.then_inc(x_filled, 1)

            expert_reg = [pe.alloc_register(name=f"expert_{k}") for k in range(XB)]

            def load_expert(n, k):
                pe.reg_load(expert_reg[k], expert_of[0:1, bass.ds(n, 1)])

            def expert(k):
                return bass.ds(pe.snap(expert_reg[k], min_val=0, max_val=E - 1), 1)

            def gate_up(n, k, first):
                pe.wait_ge(x_copied, n + 1)
                if not first:
                    pe.wait_ge(h_made, n - 1)
                e = expert(k)
                for hc in range(HC):
                    w = wgu_sb[:, e, hc].rearrange("p e m n -> p (e m n)")
                    last = nc.tensor.matmul(ps[:, 2 + k % 2, 0:2 * I], xgT[:, k % 2, hc, :], w, start=(hc == 0), stop=(hc == HC - 1))
                last.then_inc(g_filled, 1)

            def transpose_h(n, k, first):
                pe.wait_ge(h_made, n + 1)
                if not first:
                    pe.wait_ge(h_copied, n - 1)
                nc.tensor.transpose(ps[:, 4 + k % 2, 0:P], hm[:, k % 2], ident).then_inc(h_filled, 1)

            def down(n, k, first):
                pe.wait_ge(h_copied, n + 1)
                if not first:
                    pe.wait_ge(y_copied, n - 1)
                w = wed_sb[:, expert(k), :].rearrange("p e n -> p (e n)")
                nc.tensor.matmul(ps[:, 6 + k % 2, 0:H], hmT[:, k % 2], w, start=True, stop=True).then_inc(y_filled, 1)

            load_expert(0, 0)
            transpose_x(0, 0, True)
            transpose_x(1, 1, True)
            gate_up(0, 0, True)
            load_expert(1, 1)
            transpose_x(2, 2, False)
            gate_up(1, 1, True)
            load_expert(2, 2)
            transpose_h(0, 0, True)
            transpose_x(3, 3, False)
            gate_up(2, 2, False)
            load_expert(3, 3)
            transpose_h(1, 1, True)
            down(0, 0, True)
            for k in range(XB - 1):
                transpose_x(XB + k, k, False)
                gate_up(XB + k - 1, (k - 1) % XB, False)
                load_expert(XB + k, k)
                transpose_h(XB + k - 2, (k - 2) % XB, False)
                down(XB + k - 3, k + 1, k == 0)
            with pe.Fori(1, MOE_TILES // XB - 1) as g:
                for k in range(XB):
                    n = g * XB + XB - 1 + k
                    transpose_x(n, (k - 1) % XB, False)
                    gate_up(n - 1, (k - 2) % XB, False)
                    load_expert(n, (k - 1) % XB)
                    transpose_h(n - 2, (k - 3) % XB, False)
                    down(n - 3, k, False)
            n = MOE_TILES - 1
            transpose_x(n, 3, False)
            gate_up(n - 1, 2, False)
            load_expert(n, 3)
            transpose_h(n - 2, 1, False)
            down(n - 3, 0, False)
            gate_up(n, 3, False)
            transpose_h(n - 1, 2, False)
            down(n - 2, 1, False)
            transpose_h(n, 3, False)
            down(n - 1, 2, False)
            down(n, 3, False)

            pe.wait_ge(ld_l1, 16 * 6)
            pe.wait_ge(y_copied, MOE_TILES)

            def transpose_vx(i):
                pe.wait_ge(vx_ready, i + 1)
                for m in range(KR // P):
                    last = nc.tensor.transpose(ps[:, 5, m * P:(m + 1) * P], vx[:, i % 2, m * P:(m + 1) * P], ident)
                last.then_inc(vxT_filled, 1)

            def low_rank_out(i):
                pe.wait_ge(vxT_ready, i + 1)
                if i >= 2:
                    pe.wait_ge(final_ready, i - 1)
                for m in range(KR // P):
                    last = nc.tensor.matmul(ps[:, 6 + i % 2, 0:H], vxT[:, i % 2, m, :], ut_sb[:, m, :],
                                            start=(m == 0), stop=(m == KR // P - 1))
                last.then_inc(o_filled, 1)

            for i in range(NT):
                pe.wait_ge(combined, i + 1)
                if i:
                    pe.wait_ge(z_copied, i)
                for hc in range(HC):
                    last = nc.tensor.matmul(ps[:, 0, hc * P:(hc + 1) * P], h_sb[:, i, hc * P:(hc + 1) * P], wbd[:, 1, i, :],
                                            start=True, stop=True)
                last.then_inc(z_filled, 1)
                if i:
                    transpose_vx(i - 1)
                pe.wait_ge(z_copied, i + 1)
                if i:
                    pe.wait_ge(hid_ready, i)
                for hc in range(HC):
                    for dc in range(HC):
                        last = nc.tensor.matmul(ps[:, 1, hc * P:(hc + 1) * P], w1_sb[:, dc, hc * P:(hc + 1) * P],
                                                zT[:, i % 2, dc, :], start=(dc == 0), stop=(dc == HC - 1))
                last.then_inc(hid_filled, 1)
                if i >= 2:
                    pe.wait_ge(vx_ready, i - 1)
                for dc in range(HC):
                    last = nc.tensor.matmul(ps[:, 2 + i % 2, :], zT[:, i % 2, dc, :], vt_sb[:, dc, :],
                                            start=(dc == 0), stop=(dc == HC - 1))
                last.then_inc(vx_filled, 1)
                pe.wait_ge(hid_ready, i + 1)
                if i:
                    pe.wait_ge(alpha_shifted, i)
                for hc in range(HC):
                    last = nc.tensor.matmul(ps[:, 4, 0:NSUB], hT[:, i % 2, hc, :], w2_sb[:, hc, :],
                                            start=(hc == 0), stop=(hc == HC - 1))
                last.then_inc(alpha_filled, 1)
                if i:
                    low_rank_out(i - 1)
            transpose_vx(NT - 1)
            low_rank_out(NT - 1)


def layout(a):
    def g(name):
        return np.asarray(a[name])

    def feat(w, n):
        return w.reshape(HC, P, n).transpose(1, 0, 2)

    wq = g("L0_ffn_wq").reshape(HC, P, NPAIR, 2, GQ, FR, 2).transpose(1, 0, 2, 4, 6, 3, 5)
    wk = g("L0_ffn_wk").reshape(HC, P, NPAIR, 2, FR, 2).transpose(1, 0, 2, 5, 3, 4)
    return {
        "x": g("x"), "cond0": g("itok_B_1_198").reshape(NT, BT).T, "cond1": g("itok_B_0_7").reshape(NT, BT).T,
        "w_cond0": g("L0_cond_weights").reshape(-1, S), "w_cond1": g("L1_cond_weights").reshape(-1, S),
        "consts": constants(),
        "ln1": g("L0_ffn_ln1_w").reshape(HC, P).T, "ln2": g("L0_ffn_ln2_w").reshape(1, H),
        "wq": wq.reshape(P, HC, NPAIR, GQ, 2, P), "wk": wk.reshape(P, HC, NPAIR, 2, P),
        "wv": feat(g("L0_ffn_wv"), HKV * D),
        "wo": g("L0_ffn_wo").reshape(HQ, D, H).transpose(1, 0, 2),
        "gate": feat(g("L0_ffn_gate_w").T, E), "bias_e": g("L0_ffn_bias_e").reshape(1, E),
        "weg": g("L0_ffn_weg").reshape(E, HC, P, I).transpose(2, 0, 1, 3),
        "weu": g("L0_ffn_weu").reshape(E, HC, P, I).transpose(2, 0, 1, 3),
        "wed": g("L0_ffn_wed").transpose(1, 0, 2),
        "wsg": feat(g("L0_ffn_wsg"), I), "wsu": feat(g("L0_ffn_wsu"), I), "wsd": g("L0_ffn_wsd"),
        "u_t": g("L1_ffn_U").transpose(0, 2, 1).reshape(KR // P, P, H).transpose(1, 0, 2),
        "v_t": feat(g("L1_ffn_V").reshape(KR, H).T, KR),
        "w1": feat(g("L1_ffn_W1"), H), "b1": g("L1_ffn_b1").reshape(HC, P).T,
        "w2": feat(g("L1_ffn_W2"), NSUB), "b2": g("L1_ffn_b2").reshape(1, NSUB),
    }


def kernel(**inputs):
    import concourse.bacc as bacc
    from concourse.bass_utils import run_bass_kernel_spmd

    arrays = {name: np.ascontiguousarray(v) for name, v in layout(inputs).items()}
    nc = bacc.Bacc("TRN2", target_bir_lowering=False, num_devices=1)
    args = {name: nc.dram_tensor(name, v.shape, mybir.dt.from_np(v.dtype), kind="ExternalInput").ap()
            for name, v in arrays.items()}
    args["out"] = nc.dram_tensor("out", (B, S, H), mybir.dt.float32, kind="ExternalOutput").ap()
    build(nc, **args)
    r = run_bass_kernel_spmd(nc, [arrays], core_ids=[0])
    return r.results[0]["out"]
```

```python
import numpy as np
import concourse.bass as bass
from concourse import mybir
from contextlib import ExitStack

B, S, H = 32, 32, 256
TOK = B * S
P = 128
NT = TOK // P
BT = P // S
HC = H // P
HQ, HKV, D = 16, 4, 128
GQ = HQ // HKV
NPAIR = HKV // 2
FR = D // 2
NC = 2
CT = NT // NC
CW = TOK // NC
E, K, I = 32, 4, 128
NSUB = 8
R = 64
KR = NSUB * R
MOE_TILES = TOK * K // P + E
WARM_START, WARM_FIRST_NORM, WARM_FIRST_COPY, WARM_COMBINE = 40, 16, 3, 40
POOL_LANES = (1, CT + 2)
EPS = 1e-6
NORM_MIN = 1e-12
THETA = 10000.0
SM_SCALE = float(1.0 / np.sqrt(np.float32(D)))
MASKED = float(-1e9 * np.sqrt(D))
RSQRT_SEED = 1597463007.0

C_IDENT = 0
C_COS = C_IDENT + P
C_SIN = C_COS + S
C_MASK = C_SIN + 2 * S
C_TRI = C_MASK + S
C_IOTA = C_TRI + P
C_PART = C_IOTA + P
C_TOK = C_PART + 1
C_END = C_TOK + NT


def constants():
    c = np.zeros((P, C_END), np.float32)
    p = np.arange(P)
    c[:, C_IDENT:C_COS] = np.eye(P)
    inv = 1.0 / np.float32(THETA) ** (np.arange(0, D, 2, dtype=np.float32) / np.float32(D))
    ang = np.arange(S, dtype=np.float32)[None, :] * inv.astype(np.float32)[p % FR][:, None]
    c[:, C_COS:C_SIN] = np.cos(ang)
    c[:, C_SIN:C_SIN + S] = -np.sin(ang)
    c[:, C_SIN + S:C_MASK] = np.sin(ang)
    c[:, C_MASK:C_TRI] = np.where(np.arange(S)[None, :] <= (p % S)[:, None], 0.0, MASKED)
    c[:, C_TRI:C_IOTA] = p[:, None] < p[None, :]
    c[:, C_IOTA:C_PART] = np.arange(P)[None, :]
    c[:, C_PART] = p
    c[:, C_TOK:C_END] = np.arange(NT)[None, :] * P + p[:, None]
    return c


def build(nc, x, cond0, cond1, w_cond0, w_cond1, consts, ln1, ln2, wq, wk, wv, wo, gate, bias_e,
          weg, weu, wed, wsg, wsu, wsd, u_t, v_t, w1, b1, w2, b2, out):
    F32, BF16, F16 = mybir.dt.float32, mybir.dt.bfloat16, mybir.dt.float16
    I32, U32 = mybir.dt.int32, mybir.dt.uint32
    ALU, ACT, AX = mybir.AluOpType, mybir.ActivationFunctionType, mybir.AxisListType.X

    ctx = ExitStack()
    with ctx:
        def sb(name, shape, dt=F32):
            return ctx.enter_context(nc.sbuf_tensor(name, shape, dt))

        def sem(name):
            return ctx.enter_context(nc.semaphore(name))

        cst = sb("cst", [P, C_END])
        h_sb = sb("h_sb", [P, NT, H])
        xs = sb("xs", [P, NT, H])
        xT = sb("xT", [P, HC, TOK])
        subj = sb("subj", [B, 2], I32)
        wbd = sb("wbd", [P, 2, NT, P])
        ln1_sb = sb("ln1_sb", [P, HC])
        ln2_sb = sb("ln2_sb", [P, H])
        ss = sb("ss", [P, NT])
        rs = sb("rs", [P, 3, CT])
        gate_sb = sb("gate_sb", [P, HC, E])
        bias_sb = sb("bias_sb", [P, E])
        probs = sb("probs", [P, NT, E])
        biased = sb("biased", [P, NT, E])
        rt = sb("rt", [P, 3, CT])
        top = sb("top", [P, NT, 8])
        top_at = sb("top_at", [P, NT, 8], U32)
        top_f = sb("top_f", [P, NT, K])
        picked = sb("picked", [P, NT, K, E])
        tmp_ke = sb("tmp_ke", [P, CT, K, E])
        w4 = sb("w4", [P, NT, K])
        rw = sb("rw", [P, 2, NT])
        chosen = sb("chosen", [P, NT, E], BF16)
        tri = sb("tri", [P, P], BF16)
        ones = sb("ones", [P, P], BF16)
        warm = sb("warm", [P, 512], BF16)
        iota16 = sb("iota16", [P, P], F16)
        rank = sb("rank", [P, NT, E])
        rank_k = sb("rank_k", [P, NT, K])
        rank_i = sb("rank_i", [P, 2, NT, K], I32)
        lane_f = sb("lane_f", [P, NT, K])
        high_f = sb("high_f", [P, NT, K])
        first_k = sb("first_k", [P, NT, K])
        tile_f = sb("tile_f", [P, NT, K])
        slot_i = sb("slot_i", [P, NT, K], I32)
        tab = sb("tab", [P, 6, E])
        tab_i = sb("tab_i", [P, 2, E], I32)
        col = sb("col", [P, 2])
        src_i = sb("src_i", [P, MOE_TILES], I32)
        expert_of = sb("expert_of", [1, MOE_TILES], I32)
        wsg_sb = sb("wsg_sb", [P, HC, I])
        wsu_sb = sb("wsu_sb", [P, HC, I])
        wsd_sb = sb("wsd_sb", [P, H])
        sh = sb("sh", [P, CW])
        sizes = dict(wq=HC * NPAIR * GQ * 2 * P, rope=2 * 2 * 2 * CW, wk=HC * NPAIR * 2 * P, wv=HC * HKV * D,
                     q=2 * 2 * CW * GQ, k=2 * 2 * CW * 2, v=CT * HKV * D, pr=2 * 512, prT=2 * 512, wo=HQ * H, oT=HQ * CW)
        arena = sb("arena", [P, sum(sizes.values())])
        starts, at = {}, 0
        for name, size in sizes.items():
            starts[name] = at
            at += size

        def part(name):
            return arena[:, starts[name]:starts[name] + sizes[name]]

        wq_sb = part("wq").rearrange("p (c g j e n) -> p c g j e n", c=HC, g=NPAIR, j=GQ, e=2)
        wk_sb = part("wk").rearrange("p (c g e n) -> p c g e n", c=HC, g=NPAIR, e=2)
        wv_sb = part("wv").rearrange("p (c n) -> p c n", c=HC)
        wo_sb = part("wo").rearrange("p (h n) -> p h n", h=HQ)
        rope_cs = part("rope").rearrange("p (w n e t) -> p w n e t", w=2, n=2, e=2)
        rope_c, rope_s = rope_cs[:, 0], rope_cs[:, 1]
        q_sb = part("q").rearrange("p (u e b j s) -> p u e b j s", u=2, e=2, b=CT * BT, j=GQ)
        k_sb = part("k").rearrange("p (u e b g s) -> p u e b g s", u=2, e=2, b=CT * BT, g=2)
        v_sb = part("v").rearrange("p (i n) -> p i n", i=CT)
        pr = part("pr").rearrange("p (n i s b k) -> p n i s b k", n=2, i=2, s=2, b=BT)
        prT = part("prT").rearrange("p (n i s q) -> p n i s q", n=2, i=2, s=2)
        oT = [part("oT").rearrange("p (h t) -> p h t", h=HQ), arena[:, 0:HQ * CW].rearrange("p (h t) -> p h t", h=HQ)]
        assert starts["rope"] + sizes["rope"] == HQ * CW
        GU = E * HC * 2 * I
        wgu_sb = arena[:, 0:GU].rearrange("p (e c m n) -> p e c m n", e=E, c=HC, m=2)
        wed_sb = arena[:, GU:GU + E * H].rearrange("p (e n) -> p e n", e=E)
        E_LATE = HQ * CW // (HC * 2 * I)
        assert GU <= starts["k"] and GU + E * H <= starts["pr"]
        st = sb("st", [P, 2, 3, CT * BT])
        XB = 4
        x_first = arena[:, starts["oT"]:starts["oT"] + NT * H].rearrange("p (i t) -> p i t", i=NT)
        mix = arena[0:B, starts["oT"] + NT * H:starts["oT"] + NT * H + 2 * S * S].rearrange("b (m n) -> b m n", m=2)
        free = [starts["pr"]]

        def late(n):
            free[0] += n
            assert free[0] <= at
            return arena[:, free[0] - n:free[0]]

        xg = late(XB * H).rearrange("p (n t) -> p n t", n=XB)
        xgT = late(2 * H).rearrange("p (n c t) -> p n c t", n=2, c=HC)
        th = late(2 * I).rearrange("p (n t) -> p n t", n=2)
        ga = late(2 * I).rearrange("p (n t) -> p n t", n=2)
        hm = late(2 * I).rearrange("p (n t) -> p n t", n=2)
        hmT = late(2 * P).rearrange("p (n t) -> p n t", n=2)
        ye = late(XB * H).rearrange("p (n t) -> p n t", n=XB)
        yg = late(2 * K * H).rearrange("p (n k t) -> p n k t", n=2, k=K)
        zT = late(2 * H).rearrange("p (n c t) -> p n c t", n=2, c=HC)
        hT = late(2 * H).rearrange("p (n c t) -> p n c t", n=2, c=HC)
        al = late(2 * 4 * NSUB).rearrange("p (n m t) -> p n m t", n=2, m=4)
        vx = late(2 * KR).rearrange("p (n t) -> p n t", n=2)
        vxT = late(2 * KR).rearrange("p (n m t) -> p n m t", n=2, m=KR // P)
        at_lane = yg.rearrange("p n k t -> p (n k t)").bitcast(F16).rearrange("p (i k t) -> p i k t", i=NT, k=K)
        at_tile = vx.rearrange("p n t -> p (n t)").bitcast(F16).rearrange("p (i k t) -> p i k t", i=NT, k=K)
        x_again = late(NT * H).rearrange("p (i t) -> p i t", i=NT)
        ut_sb = late(KR // P * H).rearrange("p (m n) -> p m n", n=H)
        vt_sb = late(HC * KR).rearrange("p (c n) -> p c n", c=HC)
        w1_sb = late(HC * H).rearrange("p (c n) -> p c n", c=HC)
        b1_sb = late(HC)
        w2_sb = late(HC * NSUB).rearrange("p (c n) -> p c n", c=HC)
        b2_sb = late(NSUB)

        mixd = nc.dram_tensor("mixing", (2, B, S * S), F32, kind="Internal").ap()
        xd = nc.dram_tensor("normed_tokens", (TOK, H), F32, kind="Internal").ap()
        yd = nc.dram_tensor("expert_out", (MOE_TILES * P, H), F32, kind="Internal").ap()

        ps = ctx.enter_context(nc.psum_tensor("ps", [P, 8, 512], F32))

        ident = cst[:, C_IDENT:C_COS]
        cosT = cst[:, C_COS:C_SIN]
        sinT = cst[:, C_SIN:C_MASK].rearrange("p (e s) -> p e s", e=2)
        mask = cst[:, C_MASK:C_TRI]

        warm_ready = sem("warm_ready")
        ld_subj = sem("ld_subj")
        ld_first = sem("ld_first")
        ld_x = sem("ld_x")
        ld_qkv = sem("ld_qkv")
        ld_wo = sem("ld_wo")
        mix_stored = [sem(f"mix_stored{m}") for m in range(2)]
        mix_gathered = [sem(f"mix_gathered{m}") for m in range(2)]
        wbd_zeroed = sem("wbd_zeroed")
        wbd_ready = [sem(f"wbd_ready{m}") for m in range(2)]
        xT_filled = sem("xT_filled")
        xT_copied = sem("xT_copied")
        ring_filled = sem("ring_filled")
        act_freed = sem("act_freed")
        dve_freed = sem("dve_freed")
        dve_step = sem("dve_step")
        k_zeroed = sem("k_zeroed")
        rope_prod = sem("rope_prod")
        rope_done = sem("rope_done")
        scores_filled = sem("scores_filled")
        shifted = sem("shifted")
        exp_done = sem("exp_done")
        probs_ready = sem("probs_ready")
        probsT_filled = sem("probsT_filled")
        probsT_ready = sem("probsT_ready")
        pv_filled = sem("pv_filled")
        o_copied_act = sem("o_copied_act")
        o_copied_dve = sem("o_copied_dve")
        ld_router = sem("ld_router")
        ld_moe = sem("ld_moe")
        ld_again = sem("ld_again")
        ld_l1 = sem("ld_l1")
        x2T_filled = sem("x2T_filled")
        x2T_copied = sem("x2T_copied")
        x1s_ready = sem("x1s_ready")
        x2s_ready = sem("x2s_ready")
        squares_done = sem("squares_done")
        logits_shifted = sem("logits_shifted")
        logits_exp = sem("logits_exp")
        chosen_ready = sem("chosen_ready")
        tri_ready = sem("tri_ready")
        shared_tanh = sem("shared_tanh")
        lane_known = sem("lane_known")
        lanes_ready = sem("lanes_ready")
        pool_lanes_ready = sem("pool_lanes_ready")
        experts_ready = sem("experts_ready")
        tiles_ready = sem("tiles_ready")
        xn_stored = sem("xn_stored")
        sources_filled = sem("sources_filled")
        sources_ready = sem("sources_ready")
        slots_ready = sem("slots_ready")
        gathered = [sem(f"gathered{n}") for n in range(XB)]
        x_filled = sem("x_filled")
        x_copied = sem("x_copied")
        g_filled = sem("g_filled")
        tanh_done = sem("tanh_done")
        ga_made = sem("ga_made")
        h_made = sem("h_made")
        h_filled = sem("h_filled")
        h_copied = sem("h_copied")
        y_filled = sem("y_filled")
        y_copied = sem("y_copied")
        y_stored = [sem(f"y_stored{n}") for n in range(XB)]
        picked_up = [[sem(f"picked_up{n}_{k}") for k in range(K)] for n in range(2)]
        combined = sem("combined")
        z_filled = sem("z_filled")
        z_copied = sem("z_copied")
        hid_filled = sem("hid_filled")
        hid_ready = sem("hid_ready")
        alpha_filled = sem("alpha_filled")
        alpha_shifted = sem("alpha_shifted")
        alpha_exp = sem("alpha_exp")
        vx_filled = sem("vx_filled")
        vx_ready = sem("vx_ready")
        vxT_filled = sem("vxT_filled")
        vxT_ready = sem("vxT_ready")
        o_filled = sem("o_filled")
        final_ready = sem("final_ready")
        stored = sem("stored")

        units = [(c, g) for c in range(NC) for g in range(NPAIR)]
        DVE_JOBS = ("cond", "k", "q", "wo", "logits", "shared_gu", "rank", "table", "shared_y")
        jobs = [("cond", c, half) for c in range(NC) for half in range(2)] + [("xT", 0)]

        def qk_jobs(c, g):
            return [("k", c, g)] + [("q", c, g, j) for j in range(GQ)]

        def v_jobs(c):
            return [("v", c, n) for n in range(CT // 2)]

        jobs += qk_jobs(0, 0) + v_jobs(0) + qk_jobs(0, 1) + qk_jobs(1, 0) + qk_jobs(1, 1) + v_jobs(1)
        jobs += [("wo", 0, 0), ("wo", 0, 1), ("wo", 1, 0), ("logits", 0), ("wo", 1, 1), ("rank", 0), ("shared_gu", 0)]
        jobs += [("logits", 1), ("shared_y", 0), ("rank", 1), ("shared_gu", 1), ("table", 0), ("shared_y", 1)]
        place = {job: n for n, job in enumerate(jobs)}
        freed_by = {}
        count = {"act": 0, "dve": 0}
        for job in jobs:
            who = "dve" if job[0] in DVE_JOBS else "act"
            count[who] += 1
            freed_by[job] = (dve_freed if who == "dve" else act_freed, count[who])

        def slot(job):
            n = place[job] % 2
            return ps[:, 2 * n:2 * n + 2, :]

        def wait_filled(eng, job):
            eng.wait_ge(ring_filled, place[job] + 1)

        g_bank = 2 * (place["shared_y", 1] % 2)
        x_bank = 2 - g_bank

        def first_out(c):
            return slot(("xT", 0)) if c == 0 else ps[:, 4:6, :]

        ropes = [job for job in jobs if job[0] in ("k", "q")]
        rope_no = {job: n for n, job in enumerate(ropes)}

        def o_dst(c, g, n, b):
            heads = oT[c][:, 2 * g * GQ:2 * (g + 1) * GQ, :]
            return heads.rearrange("p j (n i b q) -> p n b i j q", n=2, b=BT, q=S)[:, n, b]

        def o_src(b):
            return ps[:, 4 + b, :].rearrange("p (i j q) -> p i j q", i=2, q=S)

        def half_tiles(c, half):
            return range(c * CT + half * CT // 2, c * CT + (half + 1) * CT // 2)

        def load_blocks(eng, m, quarters):
            rows = mixd[m].rearrange("(i q) (c d) -> q c i d", q=BT, c=S)
            for q in quarters:
                eng.dma_start(wbd[S * q:S * q + S, m, :, S * q:S * q + S], rows[q]).then_inc(wbd_ready[m], 16)

        block = ctx.enter_context(nc.Block())

        @block.sync
        def _(sp):
            sp.dma_start(subj[:, 0:1], cond0).then_inc(ld_subj, 16)
            sp.dma_start(subj[:, 1:2], cond1).then_inc(ld_subj, 16)
            sp.dma_start(x_first, x.rearrange("(i b) c t -> (b c) i t", b=BT)).then_inc(ld_x, 16)
            sp.dma_start(cst[:], consts).then_inc(ld_first, 16)
            sp.dma_start(ln1_sb[:], ln1).then_inc(ld_first, 16)
            sp.wait_ge(wbd_zeroed, 1)
            sp.wait_ge(mix_stored[0], 16)
            load_blocks(sp, 0, range(BT // 2, BT))
            sp.dma_start(wk_sb[:], wk).then_inc(ld_qkv, 16)
            sp.wait_ge(wbd_ready[0], 16 * BT)
            sp.dma_start(wq_sb[:], wq).then_inc(ld_qkv, 16)
            sp.dma_start(wv_sb[:], wv).then_inc(ld_qkv, 16)
            sp.dma_start(wo_sb[:], wo).then_inc(ld_wo, 16)
            for dst, src in ((gate_sb[:], gate), (bias_sb[:], bias_e.broadcast_to([P, E])),
                             (ln2_sb[:], ln2.broadcast_to([P, H])), (wsg_sb[:], wsg), (wsu_sb[:], wsu), (wsd_sb[:], wsd)):
                sp.dma_start(dst, src).then_inc(ld_router, 16)

            def load_experts(e0, e1):
                for m, w in enumerate((weg, weu)):
                    sp.dma_start(wgu_sb[:, e0:e1, :, m, :], w[:, e0:e1]).then_inc(ld_moe, 16)

            sp.wait_ge(scores_filled, 2 * len(units))
            load_experts(E_LATE, E)
            sp.wait_ge(pv_filled, 2 * len(units))
            sp.dma_start(wed_sb, wed).then_inc(ld_moe, 16)
            x_rows = xd.rearrange("(i p) t -> p i t", p=P)
            sp.wait_ge(x2s_ready, 2)
            sp.dma_start(x_rows[:, 0:CT, :], xs[:, 0:CT, :]).then_inc(xn_stored, 16)
            sp.wait_ge(*freed_by["wo", 1, 1])
            load_experts(0, E_LATE)
            sp.wait_ge(x2s_ready, 4)
            sp.dma_start(x_rows[:, CT:NT, :], xs[:, CT:NT, :]).then_inc(xn_stored, 16)
            sp.dma_start(x_again, x.rearrange("(i b) c t -> (b c) i t", b=BT)).then_inc(ld_again, 16)
            for dst, src in ((ut_sb, u_t), (vt_sb, v_t), (w1_sb, w1), (b1_sb, b1), (w2_sb, w2),
                             (b2_sb, b2.broadcast_to([P, NSUB]))):
                sp.dma_start(dst, src).then_inc(ld_l1, 16)

            def store_y(n, k):
                sp.wait_ge(y_copied, n + 1)
                sp.dma_start(yd[bass.ds(n * P, P), :], ye[:, k, :]).then_inc(y_stored[k], 16)

            with sp.Fori(0, MOE_TILES // XB) as g:
                for k in range(XB):
                    store_y(g * XB + k, k)
            o_t = out.rearrange("(i b) c t -> i (b c) t", b=BT)
            for i in range(NT):
                sp.wait_ge(final_ready, i + 1)
                sp.dma_start(o_t[i], h_sb[:, i, :]).then_inc(stored, 16)
            sp.wait_ge(stored, 16 * NT)

        @block.gpsimd
        def _(pool):
            pool.wait_ge(ld_subj, 32)
            for m, w in enumerate((w_cond0, w_cond1)):
                pool.indirect_dma_start(out=mix[:, m, :], out_offset=None, in_=w,
                                        in_offset=bass.IndirectOffsetOnAxis(ap=subj[:, m:m + 1], axis=0)
                                        ).then_inc(mix_gathered[m], 16)
            pool.wait_ge(k_zeroed, 1)
            pool.wait_ge(mix_gathered[0], 16)
            pool.wait_ge(mix_gathered[1], 16)
            for n, job in enumerate(ropes):
                kind, c, g = job[:3]
                u = units.index((c, g))
                pool.wait_ge(rope_prod, n + 1)
                if u >= 2:
                    pool.wait_ge(scores_filled, 2 * (u - 1))
                a = rope_c[:, n % 2].rearrange("p e (b s) -> p e b s", s=S)
                b = rope_s[:, n % 2].rearrange("p e (b s) -> p e b s", s=S)
                if kind == "k":
                    if n:
                        pool.wait_ge(rope_done, n)
                    for s in range(2):
                        lanes = slice(FR * s, FR * s + FR)
                        last = nc.gpsimd.tensor_tensor(k_sb[lanes, u % 2, :, :, s, :], a[lanes], b[lanes], ALU.add)
                else:
                    last = nc.gpsimd.tensor_tensor(q_sb[:, u % 2, :, :, job[3], :], a, b, ALU.add)
                last.then_inc(rope_done, 1)
                if kind == "k":
                    pool.wait_ge(rope_done, n + 1)

            for c in range(NC):
                pool.wait_ge(lane_known, c + 1)
                for i in range(POOL_LANES[c], (c + 1) * CT):
                    for k in range(K):
                        last = nc.gpsimd.tensor_scalar(at_lane[:, i, k, :], iota16[:], lane_f[:, i, k:k + 1],
                                                       cst[:, C_TOK + i:C_TOK + i + 1], ALU.is_equal, ALU.mult)
                last.then_inc(pool_lanes_ready, 1)
            pool.wait_ge(sources_ready, 1)
            pool.wait_ge(xn_stored, 32)

            for n in range(MOE_TILES):
                if n >= XB:
                    pool.wait_ge(x_filled, n - XB + 1)
                pool.indirect_dma_start(out=xg[:, n % XB, :], out_offset=None, in_=xd,
                                        in_offset=bass.IndirectOffsetOnAxis(ap=src_i[:, n:n + 1], axis=0)
                                        ).then_inc(gathered[n % XB], 16)
            pool.wait_ge(slots_ready, 1)
            for k in range(XB):
                pool.wait_ge(y_stored[k], 16 * (MOE_TILES // XB))
            for i in range(NT):
                if i >= 2:
                    pool.wait_ge(combined, i - 1)
                for k in range(K):
                    pool.indirect_dma_start(out=yg[:, i % 2, k, :], out_offset=None, in_=yd,
                                            in_offset=bass.IndirectOffsetOnAxis(ap=slot_i[:, i, k:k + 1], axis=0)
                                            ).then_inc(picked_up[i % 2][k], 16)

        @block.scalar
        def _(act):
            def mixing_matrices(m):
                act.wait_ge(mix_gathered[m], 16)
                act.dma_start(mixd[m], mix[:, m, :]).then_inc(mix_stored[m], 16)
                act.wait_ge(mix_stored[m], 16)
                load_blocks(act, m, range(0, BT // 2) if m == 0 else range(BT))

            act.wait_ge(wbd_zeroed, 1)
            mixing_matrices(0)

            def squares_first(c):
                for half in range(2):
                    act.wait_ge(*freed_by["cond", c, half])
                    for i in half_tiles(c, half):
                        last = nc.scalar.activation(xs[:, i, :], h_sb[:, i, :], ACT.Square, accum_out=ss[:, i:i + 1])
                last.then_inc(squares_done, 1)

            def copy_xT(c):
                if c == 0:
                    wait_filled(act, ("xT", 0))
                    act.wait_ge(ld_first, 32)
                else:
                    act.wait_ge(xT_filled, 1)
                for hc in range(HC):
                    last = nc.scalar.activation(xT[:, hc, c * CW:(c + 1) * CW], first_out(c)[:, hc, :], ACT.Copy,
                                                scale=ln1_sb[:, hc:hc + 1])
                last.then_inc(act_freed if c == 0 else xT_copied, 1)

            def copy_v(c):
                for n in range(CT // 2):
                    wait_filled(act, ("v", c, n))
                    nc.scalar.activation(v_sb[:, 2 * n:2 * n + 2, :], slot(("v", c, n)), ACT.Copy).then_inc(act_freed, 1)

            def exp(u, n):
                act.wait_ge(shifted, 2 * u + n + 1)
                nc.scalar.activation(pr[:, n], pr[:, n], ACT.Exp, scale=SM_SCALE).then_inc(exp_done, 1)

            def copy_probsT(u):
                for n in range(2):
                    act.wait_ge(probsT_filled, 2 * u + n + 1)
                    nc.scalar.activation(prT[:, n], ps[:, 6 + n, :].rearrange("p (i k t) -> p i k t", i=2, k=2),
                                         ACT.Copy).then_inc(probsT_ready, 1)

            def copy_o(u, n):
                c, g = units[u]
                act.wait_ge(pv_filled, 2 * u + n + 1)
                for b in range(2):
                    last = nc.scalar.activation(o_dst(c, g, n, b), o_src(b), ACT.Copy)
                last.then_inc(o_copied_act, 1)

            def squares(c, half):
                act.wait_ge(*freed_by["wo", c, half])
                for i in half_tiles(c, half):
                    last = nc.scalar.activation(xs[:, i, :], h_sb[:, i, :], ACT.Square, accum_out=ss[:, i:i + 1])
                last.then_inc(squares_done, 1)

            squares_first(0)
            copy_xT(0)
            squares_first(1)
            copy_xT(1)
            mixing_matrices(1)
            copy_v(0)
            exp(0, 0)
            exp(0, 1)
            for u in range(2):
                copy_probsT(u)
                copy_o(u, 0)
                copy_o(u, 1)
                exp(u + 1, 0)
                exp(u + 1, 1)
            copy_v(1)
            copy_probsT(2)
            exp(3, 0)
            exp(3, 1)
            copy_o(2, 0)
            copy_o(2, 1)
            copy_probsT(3)
            squares(0, 0)
            copy_o(3, 0)
            copy_o(3, 1)
            squares(0, 1)

            def copy_second(c):
                act.wait_ge(x2T_filled, c + 1)
                nc.scalar.activation(xT[:, :, c * CW:(c + 1) * CW], ps[:, 4:6, :], ACT.Copy).then_inc(x2T_copied, 1)

            def router(c):
                act.wait_ge(logits_shifted, c + 1)
                p = probs[:, c * CT:(c + 1) * CT, :]
                nc.scalar.activation(p, p, ACT.Exp).then_inc(logits_exp, 1)

            def shared_gate(c):
                wait_filled(act, ("shared_gu", c))
                if c:
                    act.wait_ge(ring_filled, place["shared_y", c - 1] + 1)
                nc.scalar.activation(sh[:], slot(("shared_gu", c))[:, 0, :], ACT.Tanh, scale=0.5).then_inc(shared_tanh, 1)

            copy_second(0)
            squares(1, 0)
            router(0)
            squares(1, 1)
            shared_gate(0)
            copy_second(1)
            router(1)
            shared_gate(1)

            def copy_x(n, k, first):
                act.wait_ge(x_filled, n + 1)
                if not first:
                    act.wait_ge(g_filled, n - 1)
                nc.scalar.activation(xgT[:, k % 2], ps[:, x_bank + k % 2, 0:H].rearrange("p (c t) -> p c t", c=HC),
                                     ACT.Copy).then_inc(x_copied, 1)

            def tanh(n, k, first):
                act.wait_ge(g_filled, n + 1)
                if not first:
                    act.wait_ge(h_made, n - 1)
                nc.scalar.activation(th[:, k % 2], ps[:, g_bank + k % 2, 0:I], ACT.Tanh, scale=0.5).then_inc(tanh_done, 1)

            def copy_y(n, k, first):
                act.wait_ge(y_filled, n + 1)
                if not first:
                    act.wait_ge(y_stored[k], (n - k) * (16 // XB))
                nc.scalar.activation(ye[:, k, :], ps[:, 6 + k % 2, 0:H], ACT.Copy).then_inc(y_copied, 1)

            copy_x(0, 0, True)
            copy_x(1, 1, True)
            tanh(0, 0, True)
            copy_x(2, 2, False)
            tanh(1, 1, True)
            copy_x(3, 3, False)
            tanh(2, 2, False)
            copy_y(0, 0, True)
            for k in range(XB - 1):
                copy_x(XB + k, k, False)
                tanh(XB + k - 1, (k - 1) % XB, False)
                copy_y(k + 1, k + 1, True)
            with act.Fori(1, MOE_TILES // XB - 1) as g:
                for k in range(XB):
                    n = g * XB + XB - 1 + k
                    copy_x(n, (k - 1) % XB, False)
                    tanh(n - 1, (k - 2) % XB, False)
                    copy_y(n - 3, k, False)
            n = MOE_TILES - 1
            copy_x(n, 3, False)
            tanh(n - 1, 2, False)
            copy_y(n - 3, 0, False)
            tanh(n, 3, False)
            copy_y(n - 2, 1, False)
            copy_y(n - 1, 2, False)
            copy_y(n, 3, False)

            act.wait_ge(ld_l1, 16 * 6)
            for i in range(NT):
                act.wait_ge(z_filled, i + 1)
                nc.scalar.activation(zT[:, i % 2], ps[:, 0, 0:H].rearrange("p (c t) -> p c t", c=HC), ACT.Copy).then_inc(z_copied, 1)
                if i:
                    act.wait_ge(vxT_filled, i)
                    nc.scalar.activation(vxT[:, (i - 1) % 2], ps[:, 5, :].rearrange("p (m t) -> p m t", t=P),
                                         ACT.Copy).then_inc(vxT_ready, 1)
                act.wait_ge(hid_filled, i + 1)
                for hc in range(HC):
                    last = nc.scalar.activation(hT[:, i % 2, hc], ps[:, 1, hc * P:(hc + 1) * P], ACT.Relu, bias=b1_sb[:, hc:hc + 1])
                last.then_inc(hid_ready, 1)
                act.wait_ge(alpha_shifted, i + 1)
                nc.scalar.activation(al[:, i % 2, 1], al[:, i % 2, 0], ACT.Exp, accum_out=al[:, i % 2, 3, 1:2]).then_inc(alpha_exp, 1)
            act.wait_ge(vxT_filled, NT)
            nc.scalar.activation(vxT[:, (NT - 1) % 2], ps[:, 5, :].rearrange("p (m t) -> p m t", t=P), ACT.Copy).then_inc(vxT_ready, 1)

        @block.vector
        def _(dve):
            step = [0]

            def link(ins):
                step[0] += 1
                ins.then_inc(dve_step, 1)
                dve.wait_ge(dve_step, step[0])

            def rsqrt_mean(tiles, v, y, t):
                link(nc.vector.tensor_scalar(v, ss[:, tiles[0]:tiles[-1] + 1], 1.0 / H, EPS, ALU.mult, ALU.add))
                link(nc.vector.tensor_scalar(y.bitcast(I32), v.bitcast(I32), -0.5, RSQRT_SEED, ALU.mult, ALU.add))
                for _ in range(3):
                    link(nc.vector.scalar_tensor_tensor(out=t, in0=y, scalar=-0.5, in1=y, op0=ALU.mult, op1=ALU.mult))
                    link(nc.vector.tensor_tensor(t, t, v, ALU.mult))
                    link(nc.vector.scalar_tensor_tensor(out=y, in0=t, scalar=1.5, in1=y, op0=ALU.add, op1=ALU.mult))

            nc.vector.memset(warm[:], 0.0).then_inc(warm_ready, 1)
            nc.vector.memset(wbd[:], 0.0).then_inc(wbd_zeroed, 1)
            nc.vector.memset(k_sb[:], 0.0).then_inc(k_zeroed, 1)
            for c in range(NC):
                for half in range(2):
                    wait_filled(dve, ("cond", c, half))
                    tiles = half_tiles(c, half)
                    nc.vector.tensor_copy(h_sb[:, tiles[0]:tiles[-1] + 1, :],
                                          slot(("cond", c, half))[:, 0, :].rearrange("p (i t) -> p i t", t=H)
                                          ).then_inc(dve_freed, 1)
                v, y, t = rs[:, 0], rs[:, 1], rs[:, 2]
                dve.wait_ge(squares_done, c + 1)
                rsqrt_mean(range(c * CT, (c + 1) * CT), v, y, t)
                for i in range(CT):
                    n = c * CT + i
                    last = nc.vector.tensor_scalar(xs[:, n, :], h_sb[:, n, :], y[:, i:i + 1], None, ALU.mult)
                last.then_inc(x1s_ready, 1)

            def rope(job):
                n = rope_no[job]
                wait_filled(dve, job)
                if n >= 2:
                    dve.wait_ge(rope_done, n - 1)
                y = slot(job).rearrange("p e (b s) -> p e b s", s=S)
                shape = [P, 2, CW // S, S]
                nc.vector.tensor_tensor(rope_c[:, n % 2].rearrange("p e (b s) -> p e b s", s=S), y,
                                        cosT[:, None, None, :].broadcast_to(shape), ALU.mult)
                ins = nc.vector.tensor_tensor(rope_s[:, n % 2].rearrange("p e (b s) -> p e b s", s=S), y[:, ::-1],
                                              sinT[:, :, None, :].broadcast_to(shape), ALU.mult)
                ins.then_inc(dve_freed, 1)
                dve.wait_ge(dve_freed, freed_by[job][1])
                dve.sem_inc(rope_prod, 1)

            def rows_of(n):
                return pr[:, n].rearrange("p i s b k -> p (i s b) k")

            def softmax_shift(u, n):
                dve.wait_ge(scores_filled, 2 * u + n + 1)
                link(nc.vector.tensor_tensor(rows_of(n), ps[:, 4 + n, :].rearrange("p (n t) -> p n t", t=S),
                                             mask[:, None, :].broadcast_to([P, CT * BT, S]), ALU.add))
                link(nc.vector.tensor_reduce(st[:, n, 0], rows_of(n), AX, ALU.max))
                nc.vector.tensor_tensor(rows_of(n), rows_of(n), st[:, n, 0, :, None].broadcast_to([P, CT * BT, S]),
                                        ALU.subtract).then_inc(shifted, 1)

            def softmax_norm(u, n):
                dve.wait_ge(exp_done, 2 * u + n + 1)
                link(nc.vector.tensor_reduce(st[:, n, 1], rows_of(n), AX, ALU.add))
                link(nc.vector.reciprocal(st[:, n, 2], st[:, n, 1]))
                nc.vector.tensor_tensor(rows_of(n), rows_of(n), st[:, n, 2, :, None].broadcast_to([P, CT * BT, S]),
                                        ALU.mult).then_inc(probs_ready, 1)

            def copy_o(u, n):
                c, g = units[u]
                dve.wait_ge(pv_filled, 2 * u + n + 1)
                for b in range(2, BT):
                    last = nc.vector.tensor_copy(o_dst(c, g, n, b), o_src(b))
                last.then_inc(o_copied_dve, 1)

            def residual(c, half):
                wait_filled(dve, ("wo", c, half))
                tiles = half_tiles(c, half)
                hc = h_sb[:, tiles[0]:tiles[-1] + 1, :]
                y = slot(("wo", c, half))[:, 0, :].rearrange("p (i t) -> p i t", t=H)
                nc.vector.tensor_tensor(hc, y, hc, ALU.add).then_inc(dve_freed, 1)

            def second_norm(c, half):
                dve.wait_ge(squares_done, NC + 2 * c + half + 1)
                if c == 0 and half == 0:
                    dve.wait_ge(ld_router, 16 * 6)
                tiles = half_tiles(c, half)
                v, y, t = (rs[:, m, 0:len(tiles)] for m in range(3))
                rsqrt_mean(tiles, v, y, t)
                for i, n in enumerate(tiles):
                    last = nc.vector.scalar_tensor_tensor(out=xs[:, n, :], in0=h_sb[:, n, :], scalar=y[:, i:i + 1],
                                                          in1=ln2_sb[:], op0=ALU.mult, op1=ALU.mult)
                last.then_inc(x2s_ready, 1)

            def router_shift(c):
                wait_filled(dve, ("logits", c))
                y = slot(("logits", c))[:, 0, 0:CT * E].rearrange("p (i e) -> p i e", e=E)
                link(nc.vector.tensor_reduce(rt[:, 0], y, AX, ALU.max))
                ins = nc.vector.tensor_tensor(probs[:, c * CT:(c + 1) * CT, :], y,
                                              rt[:, 0, :, None].broadcast_to([P, CT, E]), ALU.subtract)
                ins.then_inc(dve_freed, 1)
                dve.wait_ge(dve_freed, freed_by["logits", c][1])
                dve.sem_inc(logits_shifted, 1)

            def router_choose(c):
                tiles = slice(c * CT, (c + 1) * CT)
                p = probs[:, tiles, :]
                dve.wait_ge(logits_exp, c + 1)
                link(nc.vector.tensor_reduce(rt[:, 1], p, AX, ALU.add))
                link(nc.vector.reciprocal(rt[:, 2], rt[:, 1]))
                link(nc.vector.tensor_tensor(p, p, rt[:, 2, :, None].broadcast_to([P, CT, E]), ALU.mult))
                link(nc.vector.tensor_tensor(biased[:, tiles, :], p, bias_sb[:, None, :].broadcast_to([P, CT, E]), ALU.add))
                for i in range(c * CT, (c + 1) * CT):
                    last = nc.vector.max(top[:, i, :], biased[:, i, :])
                link(last)
                for i in range(c * CT, (c + 1) * CT):
                    last = nc.vector.max_index(top_at[:, i, :], top[:, i, :], biased[:, i, :])
                link(last)
                link(nc.vector.tensor_copy(top_f[:, tiles, :], top_at[:, tiles, 0:K]))
                flags = picked[:, tiles].rearrange("p i k e -> p (i k) e")
                link(nc.vector.tensor_tensor(flags, cst[:, None, C_IOTA:C_IOTA + E].broadcast_to([P, CT * K, E]),
                                             top_f[:, tiles, :].rearrange("p i k -> p (i k)")[:, :, None].broadcast_to([P, CT * K, E]),
                                             ALU.is_equal))
                with nc.allow_low_precision(reason="sums of flags are 0 or 1"):
                    nc.vector.tensor_reduce(chosen[:, tiles, :], picked[:, tiles].rearrange("p i k e -> p i e k"),
                                            AX, ALU.add).then_inc(chosen_ready, 1)

            def router_weights(c):
                tiles = slice(c * CT, (c + 1) * CT)
                p = probs[:, tiles, :]
                link(nc.vector.tensor_tensor(tmp_ke[:], picked[:, tiles], p[:, :, None, :].broadcast_to([P, CT, K, E]), ALU.mult))
                link(nc.vector.tensor_reduce(w4[:, tiles, :], tmp_ke[:], AX, ALU.add))
                link(nc.vector.tensor_reduce(rw[:, 0, tiles], w4[:, tiles, :], AX, ALU.add))
                link(nc.vector.tensor_scalar(rw[:, 0, tiles], rw[:, 0, tiles], NORM_MIN, None, ALU.max))
                link(nc.vector.reciprocal(rw[:, 1, tiles], rw[:, 0, tiles]))
                link(nc.vector.tensor_scalar(rw[:, 1, tiles], rw[:, 1, tiles], 0.5, None, ALU.mult))
                link(nc.vector.tensor_tensor(w4[:, tiles, :], w4[:, tiles, :],
                                             rw[:, 1, tiles, None].broadcast_to([P, CT, K]), ALU.mult))

            def shared_hidden(c):
                dve.wait_ge(shared_tanh, c + 1)
                y = slot(("shared_gu", c))
                link(nc.vector.scalar_tensor_tensor(out=sh[:], in0=sh[:], scalar=1.0, in1=y[:, 0, :], op0=ALU.add, op1=ALU.mult))
                nc.vector.scalar_tensor_tensor(out=sh[:], in0=sh[:], scalar=0.5, in1=y[:, 1, :],
                                               op0=ALU.mult, op1=ALU.mult).then_inc(dve_freed, 1)

            def ranks(c):
                tiles = slice(c * CT, (c + 1) * CT)
                wait_filled(dve, ("rank", c))
                y = slot(("rank", c))[:, 0, 0:CT * E].rearrange("p (i e) -> p i e", e=E)
                link(nc.vector.tensor_copy(rank[:, tiles, :], y))
                if c == 0:
                    dve.sem_inc(dve_freed, 1)

            def places(c):
                tiles = slice(c * CT, (c + 1) * CT)
                link(nc.vector.tensor_tensor(tmp_ke[:], picked[:, tiles], rank[:, tiles, None, :].broadcast_to([P, CT, K, E]), ALU.mult))
                link(nc.vector.tensor_reduce(rank_k[:, tiles, :], tmp_ke[:], AX, ALU.add))
                link(nc.vector.tensor_copy(rank_i[:, 0, tiles, :], rank_k[:, tiles, :]))
                link(nc.vector.tensor_scalar(rank_i[:, 1, tiles, :], rank_i[:, 0, tiles, :], P - 1, None, ALU.bitwise_and))
                ins = nc.vector.tensor_copy(lane_f[:, tiles, :], rank_i[:, 1, tiles, :])
                ins.then_inc(lane_known, 1)
                dve.wait_ge(lane_known, c + 1)
                link(nc.vector.tensor_scalar(rank_i[:, 1, tiles, :], rank_i[:, 0, tiles, :], 7, None, ALU.logical_shift_right))
                link(nc.vector.tensor_copy(high_f[:, tiles, :], rank_i[:, 1, tiles, :]))

            def lanes(i0, i1):
                for i in range(i0, i1):
                    for k in range(K):
                        last = nc.vector.tensor_scalar(at_lane[:, i, k, :], iota16[:], lane_f[:, i, k:k + 1],
                                                       cst[:, C_TOK + i:C_TOK + i + 1], ALU.is_equal, ALU.mult)
                last.then_inc(lanes_ready, 1)

            def tile_tables():
                n_e, c_e, cum, first, done, t = (tab[:, m] for m in range(6))
                link(nc.vector.tensor_copy(n_e, slot(("rank", 1))[:, 1, 0:E]))
                dve.sem_inc(dve_freed, 1)
                link(nc.vector.tensor_scalar(tab_i[:, 0], n_e, float(P - 1), None, ALU.add))
                link(nc.vector.tensor_scalar(tab_i[:, 1], tab_i[:, 0], 7, None, ALU.logical_shift_right))
                link(nc.vector.tensor_copy(c_e, tab_i[:, 1]))
                link(nc.vector.memset(t, 0.0))
                link(nc.vector.tensor_tensor_scan(cum, c_e, t, 0.0, ALU.add, ALU.add))
                link(nc.vector.tensor_tensor(first, cum, c_e, ALU.subtract))
                for c in range(NC):
                    if c == NC - 1:
                        lanes(CT, POOL_LANES[1])
                    tiles = slice(c * CT, (c + 1) * CT)
                    link(nc.vector.tensor_tensor(tmp_ke[:], picked[:, tiles],
                                                 first[:, None, None, :].broadcast_to([P, CT, K, E]), ALU.mult))
                    link(nc.vector.tensor_reduce(first_k[:, tiles, :], tmp_ke[:], AX, ALU.add))
                    link(nc.vector.tensor_tensor(tile_f[:, tiles, :], first_k[:, tiles, :], high_f[:, tiles, :], ALU.add))
                    nc.vector.tensor_tensor(at_tile[:, tiles].rearrange("p i k t -> p (i k) t"),
                                            iota16[:, None, 0:MOE_TILES].broadcast_to([P, CT * K, MOE_TILES]),
                                            tile_f[:, tiles, :].rearrange("p i k -> p (i k)")[:, :, None].broadcast_to([P, CT * K, MOE_TILES]),
                                            ALU.is_equal).then_inc(tiles_ready, 1)
                tile, mine = (col[:, m:m + 1] for m in range(2))
                link(nc.vector.tensor_scalar(tile, cum[:, E - 1:E], -1.0, cst[:, C_PART:C_PART + 1], ALU.add, ALU.min))
                link(nc.vector.tensor_scalar(done, cum, tile, None, ALU.is_le))
                nc.vector.tensor_reduce(mine, done, AX, ALU.add).then_inc(experts_ready, 1)
                shared_hidden(1)
                dve.wait_ge(sources_filled, 1)
                y = slot(("table", 0))
                nc.vector.tensor_copy(src_i[:], y[:, 0, 0:MOE_TILES]).then_inc(sources_ready, 1)
                wait_filled(dve, ("table", 0))
                nc.vector.tensor_copy(expert_of[:], y[0:1, 1, 0:MOE_TILES]).then_inc(dve_freed, 1)
                nc.vector.scalar_tensor_tensor(out=slot_i[:], in0=first_k[:], scalar=float(P), in1=rank_k[:],
                                               op0=ALU.mult, op1=ALU.add).then_inc(slots_ready, 1)

            def shared_add(c):
                wait_filled(dve, ("shared_y", c))
                hc = h_sb[:, c * CT:(c + 1) * CT, :]
                ins = nc.vector.tensor_tensor(hc, slot(("shared_y", c)).rearrange("p b (i t) -> p (b i) t", t=H), hc, ALU.add)
                ins.then_inc(dve_freed, 1)

            dve.wait_ge(ld_first, 32)
            nc.vector.memset(ones[:], 1.0)
            link(nc.vector.tensor_copy(iota16[:], cst[:, C_IOTA:C_PART]))
            nc.vector.tensor_copy(tri[:], cst[:, C_TRI:C_IOTA]).then_inc(tri_ready, 1)
            for job in qk_jobs(0, 0):
                rope(job)
            for u in range(1, len(units)):
                k_job, *q_jobs = qk_jobs(*units[u])
                if u >= 2:
                    softmax_norm(u - 2, 0)
                    softmax_norm(u - 2, 1)
                rope(k_job)
                rope(q_jobs[0])
                if u >= 2:
                    copy_o(u - 2, 0)
                rope(q_jobs[1])
                if u >= 2:
                    copy_o(u - 2, 1)
                rope(q_jobs[2])
                softmax_shift(u - 1, 0)
                rope(q_jobs[3])
                softmax_shift(u - 1, 1)
            softmax_norm(2, 0)
            softmax_norm(2, 1)
            softmax_shift(3, 0)
            softmax_shift(3, 1)
            softmax_norm(3, 0)
            copy_o(2, 0)
            softmax_norm(3, 1)
            copy_o(2, 1)
            residual(0, 0)
            second_norm(0, 0)
            copy_o(3, 0)
            copy_o(3, 1)
            residual(0, 1)
            second_norm(0, 1)
            residual(1, 0)
            second_norm(1, 0)
            router_shift(0)
            router_choose(0)
            residual(1, 1)
            ranks(0)
            second_norm(1, 1)
            shared_hidden(0)
            places(0)
            lanes(0, POOL_LANES[0])
            router_shift(1)
            router_choose(1)
            shared_add(0)
            ranks(1)
            places(1)
            tile_tables()
            shared_add(1)

            def hidden(n, k, first):
                dve.wait_ge(tanh_done, n + 1)
                g, u = ps[:, g_bank + k % 2, 0:I], ps[:, g_bank + k % 2, I:2 * I]
                nc.vector.scalar_tensor_tensor(out=ga[:, k % 2], in0=th[:, k % 2], scalar=1.0, in1=g,
                                               op0=ALU.add, op1=ALU.mult).then_inc(ga_made, 1)
                dve.wait_ge(ga_made, n + 1)
                if not first:
                    dve.wait_ge(h_filled, n - 1)
                nc.vector.tensor_tensor(hm[:, k % 2], ga[:, k % 2], u, ALU.mult).then_inc(h_made, 1)

            def copy_h(n, k, first):
                dve.wait_ge(h_filled, n + 1)
                if not first:
                    dve.wait_ge(y_filled, n - 1)
                nc.vector.tensor_copy(hmT[:, k % 2], ps[:, 4 + k % 2, 0:P]).then_inc(h_copied, 1)

            hidden(0, 0, True)
            hidden(1, 1, True)
            copy_h(0, 0, True)
            hidden(2, 2, False)
            copy_h(1, 1, True)
            for k in range(XB):
                hidden(XB - 1 + k, (k - 1) % XB, False)
                copy_h(XB - 2 + k, (k - 2) % XB, False)
            with dve.Fori(1, MOE_TILES // XB - 1) as g:
                for k in range(XB):
                    n = g * XB + XB - 1 + k
                    hidden(n, (k - 1) % XB, False)
                    copy_h(n - 1, (k - 2) % XB, False)
            hidden(MOE_TILES - 1, 3, False)
            copy_h(MOE_TILES - 2, 2, False)
            copy_h(MOE_TILES - 1, 3, False)

            def combine(i):
                for k in range(K):
                    dve.wait_ge(picked_up[i % 2][k], 16 * (i // 2 + 1))
                    ins = nc.vector.scalar_tensor_tensor(out=h_sb[:, i, :], in0=yg[:, i % 2, k, :], scalar=w4[:, i, k:k + 1],
                                                         in1=h_sb[:, i, :], op0=ALU.mult, op1=ALU.add)
                    if k < K - 1:
                        link(ins)
                ins.then_inc(combined, 1)

            def finish(i):
                dve.wait_ge(o_filled, i + 1)
                nc.vector.tensor_tensor(h_sb[:, i, :], ps[:, 6 + i % 2, 0:H], h_sb[:, i, :], ALU.add).then_inc(final_ready, 1)

            router_weights(0)
            router_weights(1)
            dve.wait_ge(ld_again, 16)
            dve.wait_ge(*freed_by["shared_y", 1])
            link(nc.vector.tensor_tensor(h_sb[:], h_sb[:], x_again, ALU.add))
            combine(0)
            for i in range(NT):
                a = al[:, i % 2]
                if i + 1 < NT:
                    combine(i + 1)
                dve.wait_ge(alpha_filled, i + 1)
                if i == 0:
                    dve.wait_ge(ld_l1, 16 * 6)
                link(nc.vector.tensor_tensor(a[:, 0], ps[:, 4, 0:NSUB], b2_sb[:], ALU.add))
                link(nc.vector.tensor_reduce(a[:, 3, 0:1], a[:, 0], AX, ALU.max))
                nc.vector.tensor_scalar(a[:, 0], a[:, 0], a[:, 3, 0:1], None, ALU.subtract).then_inc(alpha_shifted, 1)
                dve.wait_ge(alpha_exp, i + 1)
                link(nc.vector.reciprocal(a[:, 3, 2:3], a[:, 3, 1:2]))
                link(nc.vector.tensor_scalar(a[:, 2], a[:, 1], a[:, 3, 2:3], None, ALU.mult))
                dve.wait_ge(vx_filled, i + 1)
                nc.vector.tensor_tensor(vx[:, i % 2].rearrange("p (k r) -> p k r", r=R),
                                        ps[:, 2 + i % 2, :].rearrange("p (k r) -> p k r", r=R),
                                        a[:, 2, :, None].broadcast_to([P, NSUB, R]), ALU.mult).then_inc(vx_ready, 1)
                if i:
                    finish(i - 1)
            finish(NT - 1)

        @block.tensor
        def _(pe):
            def claim(job):
                n = place[job]
                if n >= 2:
                    pe.wait_ge(*freed_by[jobs[n - 2]])

            def keep_warm(n):
                for _ in range(n):
                    nc.tensor.matmul(ps[:, 7, :], warm[:, 0:P], warm[:], start=True, stop=True)

            pe.wait_ge(warm_ready, 1)
            keep_warm(WARM_START)
            pe.wait_ge(wbd_ready[0], 16 * BT)
            pe.wait_ge(ld_x, 16)
            for c in range(NC):
                for half in range(2):
                    claim(("cond", c, half))
                    y = slot(("cond", c, half))[:, 0, :].rearrange("p (i t) -> p i t", t=H)
                    for n, i in enumerate(half_tiles(c, half)):
                        last = nc.tensor.matmul(y[:, n, :], wbd[:, 0, i, :], x_first[:, i, :], start=True, stop=True)
                    last.then_inc(ring_filled, 1)
            keep_warm(WARM_FIRST_NORM)

            def transpose_first(c):
                if c == 0:
                    claim(("xT", 0))
                    pe.wait_ge(ld_first, 32)
                pe.wait_ge(x1s_ready, c + 1)
                for i in range(CT):
                    for hc in range(HC):
                        last = nc.tensor.transpose(first_out(c)[:, hc, i * P:(i + 1) * P],
                                                   xs[:, c * CT + i, hc * P:(hc + 1) * P], ident)
                last.then_inc(ring_filled if c == 0 else xT_filled, 1)

            def qk_products(job):
                c, g = job[1:3]
                if c == 0:
                    pe.wait_ge(*freed_by["xT", 0])
                claim(job)
                for e in range(2):
                    for hc in range(HC):
                        w = wk_sb[:, hc, g, e, :] if job[0] == "k" else wq_sb[:, hc, g, job[3], e, :]
                        last = nc.tensor.matmul(slot(job)[:, e, :], w, xT[:, hc, c * CW:(c + 1) * CW],
                                                start=(hc == 0), stop=(hc == HC - 1))
                        if e == 1 and hc == HC - 1:
                            last.then_inc(ring_filled, 1)
                        yield

            def products(job):
                for _ in qk_products(job):
                    pass

            def products_and_attend(job, u, n):
                attending = attend(u, n)
                for m, _ in enumerate(qk_products(job)):
                    if m >= 2:
                        for _ in range(2 * BT):
                            next(attending)

            def project_qk(u):
                k_job, *q_jobs = qk_jobs(*units[u])
                products(k_job)
                products(q_jobs[0])
                if u >= 2:
                    transpose_probs(u - 2)
                    products_and_attend(q_jobs[1], u - 2, 0)
                    products_and_attend(q_jobs[2], u - 2, 1)
                else:
                    products(q_jobs[1])
                    products(q_jobs[2])
                last_job = qk_products(q_jobs[3])
                next(last_job)
                next(last_job)
                scores(u - 1, 0)
                next(last_job)
                next(last_job)
                scores(u - 1, 1)

            def project_v(c):
                for job in v_jobs(c):
                    claim(job)
                    for n in range(2):
                        i = c * CT + 2 * job[2] + n
                        for hc in range(HC):
                            last = nc.tensor.matmul(slot(job)[:, n, :], xT[:, hc, i * P:(i + 1) * P], wv_sb[:, hc, :],
                                                    start=(hc == 0), stop=(hc == HC - 1))
                    last.then_inc(ring_filled, 1)

            def scores(u, n):
                if n == 0:
                    pe.wait_ge(rope_done, (u + 1) * (GQ + 1))
                    if u == 0:
                        pe.wait_ge(xT_copied, 1)
                    if u:
                        pe.wait_ge(o_copied_act, min(2 * u, 4))
                bank = ps[:, 4 + n, :].rearrange("p (i s b k) -> p i b s k", i=2, s=2, b=BT)
                for i in range(2):
                    for b in range(BT):
                        blk = (2 * n + i) * BT + b
                        for e in range(2):
                            last = nc.tensor.matmul(bank[:, i, b], q_sb[:, u % 2, e, blk].rearrange("p j q -> p (j q)"),
                                                    k_sb[:, u % 2, e, blk].rearrange("p s k -> p (s k)"),
                                                    start=(e == 0), stop=(e == 1))
                last.then_inc(scores_filled, 1)

            def transpose_probs(u):
                for n in range(2):
                    pe.wait_ge(probs_ready, 2 * u + n + 1)
                    if u and n == 0:
                        pe.wait_ge(o_copied_dve, 2 * u)
                    for i in range(2):
                        for s in range(2):
                            last = nc.tensor.transpose(ps[:, 6 + n, (2 * i + s) * P:(2 * i + s + 1) * P],
                                                       pr[:, n, i, s].rearrange("p b k -> p (b k)"), ident)
                    last.then_inc(probsT_filled, 1)

            def attend(u, n):
                c, g = units[u]
                if n == 0:
                    pe.wait_ge(probsT_ready, 2 * u + 2)
                    pe.wait_ge(*freed_by["v", c, CT // 2 - 1])
                    if u == 2:
                        pe.wait_ge(shifted, 2 * len(units))
                else:
                    pe.wait_ge(o_copied_act, 2 * u + 1)
                    pe.wait_ge(o_copied_dve, 2 * u + 1)
                for i in range(2):
                    for s in range(2):
                        kv = 2 * g + s
                        for b in range(BT):
                            rows = slice(S * b, S * b + S)
                            last = nc.tensor.matmul(ps[:, 4 + b, (2 * i + s) * P:(2 * i + s + 1) * P],
                                                    v_sb[rows, 2 * n + i, kv * D:(kv + 1) * D],
                                                    prT[rows, n, i, s, :], start=True, stop=True)
                            if i == 1 and s == 1 and b == BT - 1:
                                last.then_inc(pv_filled, 1)
                            yield

            def project_o(c, half, u=None, between=None):
                claim(("wo", c, half))
                if half == 0:
                    pe.wait_ge(o_copied_act, 4 * (c + 1))
                    pe.wait_ge(o_copied_dve, 4 * (c + 1))
                    if c == 0:
                        pe.wait_ge(ld_wo, 16)
                y = slot(("wo", c, half))[:, 0, :].rearrange("p (i t) -> p i t", t=H)
                for n in range(CT // 2):
                    attending = attend(u, n) if u is not None else None
                    tile = half * CT // 2 + n
                    for h in range(HQ):
                        last = nc.tensor.matmul(y[:, n, :], oT[c][:, h, tile * P:(tile + 1) * P], wo_sb[:, h, :],
                                                start=(h == 0), stop=(h == HQ - 1))
                        if n == CT // 2 - 1 and h == HQ - 1:
                            last.then_inc(ring_filled, 1)
                        if u == 3 and n == 0 and h == 1:
                            transpose_probs(u)
                        if attending is not None and 0 <= h - (6 if n == 0 else 4) < HQ // 2:
                            next(attending)
                            next(attending)
                        if between is not None and 5 <= n * HQ + h < 5 + CT * HC:
                            next(between)

            def transpose_second(c):
                for i in range(CT):
                    if i % (CT // 2) == 0:
                        pe.wait_ge(x2s_ready, 2 * c + 1 + i // (CT // 2))
                    for hc in range(HC):
                        last = nc.tensor.transpose(ps[:, 4 + hc, i * P:(i + 1) * P],
                                                   xs[:, c * CT + i, hc * P:(hc + 1) * P], ident)
                last.then_inc(x2T_filled, 1)

            def router(c):
                pe.wait_ge(x2T_copied, c + 1)
                if c == 0:
                    pe.wait_ge(ld_router, 16 * 6)
                claim(("logits", c))
                for i in range(CT):
                    n = c * CT + i
                    for hc in range(HC):
                        last = nc.tensor.matmul(slot(("logits", c))[:, 0, i * E:(i + 1) * E], xT[:, hc, n * P:(n + 1) * P],
                                                gate_sb[:, hc, :], start=(hc == 0), stop=(hc == HC - 1))
                        if i == CT - 1 and hc == HC - 1:
                            last.then_inc(ring_filled, 1)
                        yield

            def shared_gate_up(c):
                claim(("shared_gu", c))
                for m, w in enumerate((wsg_sb, wsu_sb)):
                    for hc in range(HC):
                        last = nc.tensor.matmul(slot(("shared_gu", c))[:, m, :], w[:, hc, :], xT[:, hc, c * CW:(c + 1) * CW],
                                                start=(hc == 0), stop=(hc == HC - 1))
                last.then_inc(ring_filled, 1)

            def ranks(c):
                claim(("rank", c))
                pe.wait_ge(chosen_ready, c + 1)
                if c == 0:
                    pe.wait_ge(tri_ready, 1)
                for i in range(CT):
                    n = c * CT + i
                    y = slot(("rank", c))[:, 0, i * E:(i + 1) * E]
                    last = nc.tensor.matmul(y, tri[:], chosen[:, n, :], start=True, stop=(n == 0))
                    for m in range(n):
                        last = nc.tensor.matmul(y, ones[:], chosen[:, m, :], start=False, stop=(m == n - 1))
                if c == NC - 1:
                    for m in range(NT):
                        last = nc.tensor.matmul(slot(("rank", c))[:, 1, 0:E], ones[:], chosen[:, m, :],
                                                start=(m == 0), stop=(m == NT - 1))
                last.then_inc(ring_filled, 1)

            def shared_out(c):
                claim(("shared_y", c))
                pe.wait_ge(*freed_by["shared_gu", c])
                y = slot(("shared_y", c)).rearrange("p b (i t) -> p (b i) t", t=H)
                for i in range(CT):
                    last = nc.tensor.matmul(y[:, i, :], sh[:, i * P:(i + 1) * P], wsd_sb[:], start=True, stop=True)
                last.then_inc(ring_filled, 1)

            transpose_first(0)
            keep_warm(WARM_FIRST_COPY)
            pe.wait_ge(ld_qkv, 48)
            for n, job in enumerate(qk_jobs(0, 0)):
                if n == 2:
                    transpose_first(1)
                products(job)
            project_v(0)
            for u in range(1, len(units)):
                project_qk(u)
            project_v(1)
            transpose_probs(2)
            scores(3, 0)
            scores(3, 1)
            project_o(0, 0, u=2)
            project_o(0, 1, u=3)
            project_o(1, 0)
            transpose_second(0)
            project_o(1, 1, between=router(0))
            ranks(0)
            shared_gate_up(0)
            transpose_second(1)
            for _ in router(1):
                pass
            shared_out(0)
            ranks(1)
            shared_gate_up(1)
            claim(("table", 0))
            M = MOE_TILES
            for c in range(NC):
                pe.wait_ge(lanes_ready, c + 1)
                pe.wait_ge(pool_lanes_ready, c + 1)
                pe.wait_ge(tiles_ready, c + 1)
                for i in range(c * CT, (c + 1) * CT):
                    for k in range(K):
                        last = nc.tensor.matmul(slot(("table", 0))[:, 0, 0:M], at_lane[:, i, k, :], at_tile[:, i, k, :],
                                                start=(i == 0 and k == 0), stop=(i == NT - 1 and k == K - 1))
            last.then_inc(sources_filled, 1)
            pe.wait_ge(experts_ready, 1)
            nc.tensor.transpose(slot(("table", 0))[0:1, 1, 0:M], col[0:M, 1:2], ident[0:M, 0:M]).then_inc(ring_filled, 1)
            shared_out(1)

            pe.wait_ge(ld_moe, 16 * 5)
            pe.wait_ge(*freed_by["table", 0])

            def transpose_x(n, k, first):
                pe.wait_ge(gathered[k], (n - k) * (16 // XB) + 16)
                if not first:
                    pe.wait_ge(x_copied, n - 1)
                for hc in range(HC):
                    last = nc.tensor.transpose(ps[:, x_bank + k % 2, hc * P:(hc + 1) * P], xg[:, k, hc * P:(hc + 1) * P], ident)
                last.then_inc(x_filled, 1)

            expert_reg = [pe.alloc_register(name=f"expert_{k}") for k in range(XB)]

            def load_expert(n, k):
                pe.reg_load(expert_reg[k], expert_of[0:1, bass.ds(n, 1)])

            def expert(k):
                return bass.ds(pe.snap(expert_reg[k], min_val=0, max_val=E - 1), 1)

            def gate_up(n, k, first):
                pe.wait_ge(x_copied, n + 1)
                if not first:
                    pe.wait_ge(h_made, n - 1)
                e = expert(k)
                for hc in range(HC):
                    w = wgu_sb[:, e, hc].rearrange("p e m n -> p (e m n)")
                    last = nc.tensor.matmul(ps[:, g_bank + k % 2, 0:2 * I], xgT[:, k % 2, hc, :], w, start=(hc == 0), stop=(hc == HC - 1))
                last.then_inc(g_filled, 1)

            def transpose_h(n, k, first):
                pe.wait_ge(h_made, n + 1)
                if not first:
                    pe.wait_ge(h_copied, n - 1)
                nc.tensor.transpose(ps[:, 4 + k % 2, 0:P], hm[:, k % 2], ident).then_inc(h_filled, 1)

            def down(n, k, first):
                pe.wait_ge(h_copied, n + 1)
                if not first:
                    pe.wait_ge(y_copied, n - 1)
                w = wed_sb[:, expert(k), :].rearrange("p e n -> p (e n)")
                nc.tensor.matmul(ps[:, 6 + k % 2, 0:H], hmT[:, k % 2], w, start=True, stop=True).then_inc(y_filled, 1)

            load_expert(0, 0)
            transpose_x(0, 0, True)
            transpose_x(1, 1, True)
            pe.wait_ge(*freed_by["shared_y", 1])
            gate_up(0, 0, True)
            load_expert(1, 1)
            transpose_x(2, 2, False)
            gate_up(1, 1, True)
            load_expert(2, 2)
            transpose_h(0, 0, True)
            transpose_x(3, 3, False)
            gate_up(2, 2, False)
            load_expert(3, 3)
            transpose_h(1, 1, True)
            down(0, 0, True)
            for k in range(XB - 1):
                transpose_x(XB + k, k, False)
                gate_up(XB + k - 1, (k - 1) % XB, False)
                load_expert(XB + k, k)
                transpose_h(XB + k - 2, (k - 2) % XB, False)
                down(XB + k - 3, k + 1, k == 0)
            with pe.Fori(1, MOE_TILES // XB - 1) as g:
                for k in range(XB):
                    n = g * XB + XB - 1 + k
                    transpose_x(n, (k - 1) % XB, False)
                    gate_up(n - 1, (k - 2) % XB, False)
                    load_expert(n, (k - 1) % XB)
                    transpose_h(n - 2, (k - 3) % XB, False)
                    down(n - 3, k, False)
            n = MOE_TILES - 1
            transpose_x(n, 3, False)
            gate_up(n - 1, 2, False)
            load_expert(n, 3)
            transpose_h(n - 2, 1, False)
            down(n - 3, 0, False)
            gate_up(n, 3, False)
            transpose_h(n - 1, 2, False)
            down(n - 2, 1, False)
            transpose_h(n, 3, False)
            down(n - 1, 2, False)
            down(n, 3, False)

            pe.wait_ge(ld_l1, 16 * 6)
            pe.wait_ge(wbd_ready[1], 16 * BT)
            pe.wait_ge(y_copied, MOE_TILES)
            keep_warm(WARM_COMBINE)

            def transpose_vx(i):
                pe.wait_ge(vx_ready, i + 1)
                for m in range(KR // P):
                    last = nc.tensor.transpose(ps[:, 5, m * P:(m + 1) * P], vx[:, i % 2, m * P:(m + 1) * P], ident)
                last.then_inc(vxT_filled, 1)

            def low_rank_out(i):
                pe.wait_ge(vxT_ready, i + 1)
                if i >= 2:
                    pe.wait_ge(final_ready, i - 1)
                for m in range(KR // P):
                    last = nc.tensor.matmul(ps[:, 6 + i % 2, 0:H], vxT[:, i % 2, m, :], ut_sb[:, m, :],
                                            start=(m == 0), stop=(m == KR // P - 1))
                last.then_inc(o_filled, 1)

            for i in range(NT):
                pe.wait_ge(combined, i + 1)
                if i:
                    pe.wait_ge(z_copied, i)
                for hc in range(HC):
                    last = nc.tensor.matmul(ps[:, 0, hc * P:(hc + 1) * P], h_sb[:, i, hc * P:(hc + 1) * P], wbd[:, 1, i, :],
                                            start=True, stop=True)
                last.then_inc(z_filled, 1)
                if i:
                    transpose_vx(i - 1)
                pe.wait_ge(z_copied, i + 1)
                if i:
                    pe.wait_ge(hid_ready, i)
                for hc in range(HC):
                    for dc in range(HC):
                        last = nc.tensor.matmul(ps[:, 1, hc * P:(hc + 1) * P], w1_sb[:, dc, hc * P:(hc + 1) * P],
                                                zT[:, i % 2, dc, :], start=(dc == 0), stop=(dc == HC - 1))
                last.then_inc(hid_filled, 1)
                if i >= 2:
                    pe.wait_ge(vx_ready, i - 1)
                for dc in range(HC):
                    last = nc.tensor.matmul(ps[:, 2 + i % 2, :], zT[:, i % 2, dc, :], vt_sb[:, dc, :],
                                            start=(dc == 0), stop=(dc == HC - 1))
                last.then_inc(vx_filled, 1)
                pe.wait_ge(hid_ready, i + 1)
                if i:
                    pe.wait_ge(alpha_shifted, i)
                for hc in range(HC):
                    last = nc.tensor.matmul(ps[:, 4, 0:NSUB], hT[:, i % 2, hc, :], w2_sb[:, hc, :],
                                            start=(hc == 0), stop=(hc == HC - 1))
                last.then_inc(alpha_filled, 1)
                if i:
                    low_rank_out(i - 1)
            transpose_vx(NT - 1)
            low_rank_out(NT - 1)


def layout(a):
    def g(name):
        return np.asarray(a[name])

    def feat(w, n):
        return w.reshape(HC, P, n).transpose(1, 0, 2)

    wq = g("L0_ffn_wq").reshape(HC, P, NPAIR, 2, GQ, FR, 2).transpose(1, 0, 2, 4, 6, 3, 5)
    wk = g("L0_ffn_wk").reshape(HC, P, NPAIR, 2, FR, 2).transpose(1, 0, 2, 5, 3, 4)
    return {
        "x": g("x"), "cond0": g("itok_B_1_198").reshape(B, 1), "cond1": g("itok_B_0_7").reshape(B, 1),
        "w_cond0": g("L0_cond_weights").reshape(-1, S * S), "w_cond1": g("L1_cond_weights").reshape(-1, S * S),
        "consts": constants(),
        "ln1": g("L0_ffn_ln1_w").reshape(HC, P).T, "ln2": g("L0_ffn_ln2_w").reshape(1, H),
        "wq": wq.reshape(P, HC, NPAIR, GQ, 2, P), "wk": wk.reshape(P, HC, NPAIR, 2, P),
        "wv": feat(g("L0_ffn_wv"), HKV * D),
        "wo": g("L0_ffn_wo").reshape(HQ, D, H).transpose(1, 0, 2),
        "gate": feat(g("L0_ffn_gate_w").T, E), "bias_e": g("L0_ffn_bias_e").reshape(1, E),
        "weg": g("L0_ffn_weg").reshape(E, HC, P, I).transpose(2, 0, 1, 3),
        "weu": g("L0_ffn_weu").reshape(E, HC, P, I).transpose(2, 0, 1, 3),
        "wed": g("L0_ffn_wed").transpose(1, 0, 2),
        "wsg": feat(g("L0_ffn_wsg"), I), "wsu": feat(g("L0_ffn_wsu"), I), "wsd": g("L0_ffn_wsd"),
        "u_t": g("L1_ffn_U").transpose(0, 2, 1).reshape(KR // P, P, H).transpose(1, 0, 2),
        "v_t": feat(g("L1_ffn_V").reshape(KR, H).T, KR),
        "w1": feat(g("L1_ffn_W1"), H), "b1": g("L1_ffn_b1").reshape(HC, P).T,
        "w2": feat(g("L1_ffn_W2"), NSUB), "b2": g("L1_ffn_b2").reshape(1, NSUB),
    }


def kernel(**inputs):
    import concourse.bacc as bacc
    from concourse.bass_utils import run_bass_kernel_spmd

    arrays = {name: np.ascontiguousarray(v) for name, v in layout(inputs).items()}
    nc = bacc.Bacc("TRN2", target_bir_lowering=False, num_devices=1)
    args = {name: nc.dram_tensor(name, v.shape, mybir.dt.from_np(v.dtype), kind="ExternalInput").ap()
            for name, v in arrays.items()}
    args["out"] = nc.dram_tensor("out", (B, S, H), mybir.dt.float32, kind="ExternalOutput").ap()
    build(nc, **args)
    r = run_bass_kernel_spmd(nc, [arrays], core_ids=[0])
    return r.results[0]["out"]
```
